# Optimizing a Trainium2 kernel written in Bass

```python
import numpy as np
import jax
import jax.numpy as jnp

def _softmax(x, axis=-1):
    return jax.nn.softmax(x, axis=axis)

def _gelu(x):
    return jax.nn.gelu(x, approximate=True)

def _silu(x):
    return jax.nn.silu(x)

def _sigmoid(x):
    return jax.nn.sigmoid(x)

def _layernorm(x, axis=-1, eps=1e-05):
    m = jnp.mean(x, axis=axis, keepdims=True)
    v = jnp.var(x, axis=axis, keepdims=True)
    return (x - m) / jnp.sqrt(v + eps)

def _scatter_add(tgt, idx, src, axis=0):
    return tgt.at[idx].add(src)

def _segment_sum(src, seg, n):
    return jax.ops.segment_sum(src, seg, n)
kernel_name = 'mk_decoder_preln_d1_seqx_r8_84b222'

def setup_inputs(seed: int=0):
    np.random.seed(seed)
    _w = jnp.asarray

    def _rec_inputs():
        import jax
        import jax.numpy as jnp
        _rk = jax.random.key(seed)
        x = 7.22e-05 + 1 * jax.random.normal(jax.random.fold_in(_rk, 1), (4, 256, 256), jnp.float32)
        _lenS = 256 - jax.random.randint(jax.random.fold_in(_rk, 7), (4,), 0, max(1, 256 // 4) + 1, jnp.int32)
        _lenS2 = 256 - jax.random.randint(jax.random.fold_in(_rk, 8), (4,), 0, max(1, 256 // 4) + 1, jnp.int32)
        _ctx_1024P = jax.random.normal(jax.random.fold_in(_rk, 11), (4, 16, 128), jnp.float32)
        _ctx_1024c = jax.random.dirichlet(jax.random.fold_in(_rk, 511), 0.3 * jnp.ones((16,), jnp.float32), (4, 256))
        _ctx_1024t = jnp.einsum('bsk,bkd->bsd', _ctx_1024c, _ctx_1024P)
        _ctx_1024t = _ctx_1024t * jax.lax.rsqrt(jnp.mean(jnp.square(_ctx_1024t)) + 1e-12) * 0.953939
        ctx_1024 = 2.81802e-05 + 1.00001 * (_ctx_1024t + 0.3 * jax.random.normal(jax.random.fold_in(_rk, 611), (4, 256, 128), jnp.float32))
        return (x, ctx_1024)
    x, ctx_1024 = _rec_inputs()

    def _L0_attn_setup():
        import jax, jax.numpy as jnp
        import numpy as np
        HIDDEN = 256
        NUM_HEADS = 16
        NUM_KV_HEADS = 4
        HEAD_DIM = HIDDEN // NUM_HEADS
        Q_PER_KV = NUM_HEADS // NUM_KV_HEADS
        GROUP_SIZE = (Q_PER_KV + 2) * HEAD_DIM
        TOTAL_PROJ = NUM_KV_HEADS * GROUP_SIZE
        SEQ, BATCH = (256, 2)
        key = jax.random.key(seed)
        k1, k2, k3 = jax.random.split(key, 3)
        x = jax.random.normal(k1, (SEQ, BATCH, HIDDEN), dtype=jnp.float32)
        weight_qkv = jax.random.normal(k2, (TOTAL_PROJ, HIDDEN), dtype=jnp.float32) * 0.02
        weight_proj = jax.random.normal(k3, (HIDDEN, NUM_HEADS * HEAD_DIM), dtype=jnp.float32) * 0.02
        return {'x': x, 'weight_qkv': weight_qkv, 'weight_proj': weight_proj}
    _L0_attn_all = _L0_attn_setup()
    _L0_attn_in = {k: v for k, v in _L0_attn_all.items() if k in ('weight_qkv', 'weight_proj')}
    del _L0_attn_all

    def _L0_xattn_setup():
        import jax, jax.numpy as jnp
        import numpy as np
        key = jax.random.key(seed)
        ks = jax.random.split(key, 6)
        B, L, N, C, D = (8, 64, 256, 128, 128)
        return {'teacher_logits': jax.random.normal(ks[0], (B, L, N), dtype=jnp.float32), 'teacher_features': jax.random.normal(ks[1], (B, N, C), dtype=jnp.float32), 'Wq': jax.random.normal(ks[2], (D, C), dtype=jnp.float32) * (1.0 / np.sqrt(C)), 'bq': jnp.zeros((D,), dtype=jnp.float32), 'Wk': jax.random.normal(ks[3], (D, C), dtype=jnp.float32) * (1.0 / np.sqrt(C)), 'bk': jnp.zeros((D,), dtype=jnp.float32)}
    _L0_xattn_all = _L0_xattn_setup()
    _L0_xattn_in = {k: v for k, v in _L0_xattn_all.items() if k in ('Wq', 'bq', 'Wk', 'bk')}
    del _L0_xattn_all

    def _L0_ffn_setup():
        import jax, jax.numpy as jnp
        import numpy as np
        FP8_MAX = 448.0
        GLOBAL_DIV = 448.0 * 6.0

        def _fp8(x):
            return x.astype(jnp.float8_e4m3fn).astype(jnp.float32)

        def _reorder_quantize_x(x, idx):
            scale = jnp.max(jnp.abs(x)) / GLOBAL_DIV
            xr = (x / scale)[:, idx]
            scale_x = jnp.max(jnp.abs(xr), axis=1, keepdims=True) / FP8_MAX
            qx = _fp8(xr / scale_x)
            return (qx, scale_x, scale)

        def _qlinear(qx, scale_x, scale, W, idx, out_idx=None):
            Wr = W[:, idx]
            w_scale = jnp.max(jnp.abs(Wr), axis=1, keepdims=True) / FP8_MAX
            qw = _fp8(Wr / w_scale)
            y = qx * scale_x @ (qw * w_scale).T * scale
            if out_idx is not None:
                y = y[:, out_idx]
            return y
        key = jax.random.key(seed)
        ks = jax.random.split(key, 6)
        B, S, H, I = (2, 128, 256, 704)
        return {'x': jax.random.normal(ks[0], (B, S, H), jnp.float32), 'w_gate': jax.random.normal(ks[1], (I, H), jnp.float32) * 0.02, 'w_up': jax.random.normal(ks[2], (I, H), jnp.float32) * 0.02, 'w_down': jax.random.normal(ks[3], (H, I), jnp.float32) * 0.02, 'up_reorder_index': jax.random.permutation(ks[4], jnp.arange(H, dtype=jnp.int64)), 'down_reorder_index': jax.random.permutation(ks[5], jnp.arange(I, dtype=jnp.int64))}
    _L0_ffn_all = _L0_ffn_setup()
    _L0_ffn_in = {k: v for k, v in _L0_ffn_all.items() if k in ('w_gate', 'w_up', 'w_down', 'up_reorder_index', 'down_reorder_index')}
    del _L0_ffn_all
    return {'x': x, 'ctx_1024': ctx_1024, 'L0_attn_weight_qkv': _L0_attn_in['weight_qkv'], 'L0_attn_weight_proj': _L0_attn_in['weight_proj'], 'L0_xattn_Wq': _L0_xattn_in['Wq'], 'L0_xattn_bq': _L0_xattn_in['bq'], 'L0_xattn_Wk': _L0_xattn_in['Wk'], 'L0_xattn_bk': _L0_xattn_in['bk'], 'L0_ffn_w_gate': _L0_ffn_in['w_gate'], 'L0_ffn_w_up': _L0_ffn_in['w_up'], 'L0_ffn_w_down': _L0_ffn_in['w_down'], 'L0_ffn_up_reorder_index': _L0_ffn_in['up_reorder_index'], 'L0_ffn_down_reorder_index': _L0_ffn_in['down_reorder_index']}

def reference(x, ctx_1024, L0_attn_weight_qkv, L0_attn_weight_proj, L0_xattn_Wq, L0_xattn_bq, L0_xattn_Wk, L0_xattn_bk, L0_ffn_w_gate, L0_ffn_w_up, L0_ffn_w_down, L0_ffn_up_reorder_index, L0_ffn_down_reorder_index):
    import jax
    import jax.numpy as jnp

    def _L0_attn_ref(x, weight_qkv, weight_proj):
        import jax, jax.numpy as jnp
        import numpy as np
        HIDDEN = 256
        NUM_HEADS = 16
        NUM_KV_HEADS = 4
        HEAD_DIM = HIDDEN // NUM_HEADS
        Q_PER_KV = NUM_HEADS // NUM_KV_HEADS
        GROUP_SIZE = (Q_PER_KV + 2) * HEAD_DIM
        TOTAL_PROJ = NUM_KV_HEADS * GROUP_SIZE
        SEQ, BATCH = (256, 2)
        seq, batch, hidden = x.shape
        q_size = Q_PER_KV * HEAD_DIM
        qkv = x.reshape(-1, hidden) @ weight_qkv.T
        qkv = qkv.reshape(-1, NUM_KV_HEADS, GROUP_SIZE)
        q = qkv[:, :, :q_size].reshape(seq, batch, NUM_HEADS, HEAD_DIM)
        k = qkv[:, :, q_size:q_size + HEAD_DIM].reshape(seq, batch, NUM_KV_HEADS, HEAD_DIM)
        v = qkv[:, :, q_size + HEAD_DIM:].reshape(seq, batch, NUM_KV_HEADS, HEAD_DIM)
        k = jnp.repeat(k, Q_PER_KV, axis=2)
        v = jnp.repeat(v, Q_PER_KV, axis=2)
        q = q.transpose(1, 2, 0, 3)
        k = k.transpose(1, 2, 0, 3)
        v = v.transpose(1, 2, 0, 3)
        scale = 1.0 / np.sqrt(HEAD_DIM)
        scores = jnp.einsum('bhqd,bhkd->bhqk', q, k) * scale
        causal = jnp.tril(jnp.ones((seq, seq), dtype=bool))
        scores = jnp.where(causal, scores, jnp.float32(-jnp.inf))
        probs = jax.nn.softmax(scores, axis=-1)
        attn = jnp.einsum('bhqk,bhkd->bhqd', probs, v)
        attn = attn.transpose(2, 0, 1, 3).reshape(seq * batch, NUM_HEADS * HEAD_DIM)
        out = attn @ weight_proj.T
        return out.reshape(seq, batch, hidden)

    def _L0_xattn_ref(teacher_logits, teacher_features, Wq, bq, Wk, bk):
        import jax, jax.numpy as jnp
        import numpy as np
        query = jnp.einsum('bnc,dc->bnd', teacher_features, Wq) + bq
        key = jnp.einsum('bnc,dc->bnd', teacher_features, Wk) + bk
        energy = jnp.einsum('bnd,bmd->bnm', query, key)
        attention = jax.nn.softmax(energy, axis=-1)
        x_m = jnp.einsum('bln,bmn->blm', teacher_logits, attention)
        return x_m

    def _L0_ffn_ref(x, w_gate, w_up, w_down, up_reorder_index, down_reorder_index):
        import jax, jax.numpy as jnp
        import numpy as np
        FP8_MAX = 448.0
        GLOBAL_DIV = 448.0 * 6.0

        def _fp8(x):
            return x.astype(jnp.float8_e4m3fn).astype(jnp.float32)

        def _reorder_quantize_x(x, idx):
            scale = jnp.max(jnp.abs(x)) / GLOBAL_DIV
            xr = (x / scale)[:, idx]
            scale_x = jnp.max(jnp.abs(xr), axis=1, keepdims=True) / FP8_MAX
            qx = _fp8(xr / scale_x)
            return (qx, scale_x, scale)

        def _qlinear(qx, scale_x, scale, W, idx, out_idx=None):
            Wr = W[:, idx]
            w_scale = jnp.max(jnp.abs(Wr), axis=1, keepdims=True) / FP8_MAX
            qw = _fp8(Wr / w_scale)
            y = qx * scale_x @ (qw * w_scale).T * scale
            if out_idx is not None:
                y = y[:, out_idx]
            return y
        B, S, H = x.shape
        xf = x.reshape(B * S, H)
        qx, sx, sc = _reorder_quantize_x(xf, up_reorder_index)
        g = _qlinear(qx, sx, sc, w_gate, up_reorder_index, out_idx=down_reorder_index)
        u = _qlinear(qx, sx, sc, w_up, up_reorder_index, out_idx=down_reorder_index)
        t = jax.nn.silu(g) * u
        qt, st, sct = _reorder_quantize_x(t, down_reorder_index)
        y = _qlinear(qt, st, sct, w_down, down_reorder_index)
        return y.reshape(B, S, H)
    x = x + _L0_attn_ref(_layernorm(x, axis=-1), L0_attn_weight_qkv, L0_attn_weight_proj)
    x = x + _L0_xattn_ref(_layernorm(x, axis=-1), ctx_1024, L0_xattn_Wq, L0_xattn_bq, L0_xattn_Wk, L0_xattn_bk)
    x = x + _L0_ffn_ref(_layernorm(x, axis=-1), L0_ffn_w_gate, L0_ffn_w_up, L0_ffn_w_down, L0_ffn_up_reorder_index, L0_ffn_down_reorder_index)
    return x

_drawn_inputs = setup_inputs


def setup_inputs(seed=0):
    import zlib

    import numpy as np

    out = dict(_drawn_inputs(seed))
    spreads = {'L0_xattn_bq': (0.0, 0.1), 'L0_xattn_bk': (0.0, 0.1)}
    factors = {}
    for name, (base, spread) in spreads.items():
        noise = np.random.default_rng([zlib.crc32(name.encode()), seed]).standard_normal(out[name].shape)
        drawn = base * np.exp(spread * noise) if base else spread * noise
        out[name] = jnp.asarray(drawn.astype(out[name].dtype))
    for name, factor in factors.items():
        out[name] = (out[name] * factor).astype(out[name].dtype)
    return out
```

```python
import concourse.bass as bass
from concourse import mybir
from contextlib import ExitStack


def decoder_layer_kernel(nc, x, ctx_feat, w_qkv, w_proj, w_q, b_q, w_k, b_k,
                         w_gate, w_up, w_down, down_index, out):
    F32, BF16, I32 = mybir.dt.float32, mybir.dt.bfloat16, mybir.dt.int32
    ALU, ACT, AX = mybir.AluOpType, mybir.ActivationFunctionType, mybir.AxisListType

    P = 128
    SEQ, BATCH, HID = x.shape
    HALVES = BATCH // P
    NT = SEQ * HALVES
    KC = HID // P
    HD, KVH, QPK = 16, 4, 4
    HEADS = KVH * QPK
    KVD = KVH * HD
    QKV = HID + 2 * KVD
    PAIRS = SEQ * (SEQ + 1) // 2
    CD = ctx_feat.shape[2]
    CTXT = ctx_feat.shape[1] // P
    FF = w_gate.shape[0]
    FT = -(-FF // P)
    FLAST = FF - (FT - 1) * P
    FPAD = FT * P
    FH = FF // 2
    EPS = 1e-5
    FP8_MAX = 448.0
    SCALE = HD ** -0.5
    SHIFT = 2.0 ** 20
    EXP_BITS, HALF_BIT = 0x7F800000, 0x00400000
    M_LEAST = 1.5 * 2.0 ** 14

    first_pair = [q * (q + 1) // 2 for q in range(SEQ)]

    es = ExitStack()
    with es:
        def sb(name, shape, dt=F32):
            return es.enter_context(nc.sbuf_tensor(name, shape, dt))

        def sem(name):
            return es.enter_context(nc.semaphore(name))

        x_sb = sb("x_sb", [P, NT, HID])
        x1_sb = sb("x1_sb", [P, NT, HID])
        x2_sb = x1_sb
        z1_sb = sb("z1_sb", [P, NT, HID])
        z2_sb = sb("z2_sb", [P, NT, HID])
        z3_sb = z1_sb
        z1T = sb("z1T", [P, KC, NT * P])
        z2T = z1T
        ctx_sb = sb("ctx_sb", [P, SEQ * CTXT, CD])
        ctxT = sb("ctxT", [P, SEQ * CTXT * P])
        wqkv_sb = sb("wqkv_sb", [P, QKV // P, HID])
        wqkvT = sb("wqkvT", [P, KC, QKV])
        wproj_sb = sb("wproj_sb", [P, KC, HID])
        wprojT = sb("wprojT", [P, KC, HID])
        wx_sb = sb("wx_sb", [P, 2, CD])
        wxT = sb("wxT", [P, 2, CD])
        bx_sb = sb("bx_sb", [P, 2])
        qkT = sb("qkT", [P, 2, SEQ * CTXT * P])
        kv_sb = sb("kv_sb", [P, NT, 2 * KVD])
        area = sb("area", [P, 3 * PAIRS * HID])
        prod = area[:, 0:PAIRS * HID].rearrange("p (k i) -> p k i", k=PAIRS)
        pv = area[:, PAIRS * HID:].rearrange("p (h k i) -> p h k i", h=HALVES, k=PAIRS)
        g1, u1, sg, t_big = (area[:, i * 2 * FF:(i + 1) * 2 * FF].rearrange("p (b j) -> p b j", b=2)
                             for i in range(4))
        sc = sb("sc", [P, HALVES, SEQ, SEQ, HEADS])
        e_sb = sb("e_sb", [P, HALVES, SEQ, SEQ, HEADS])
        sc_max = sb("sc_max", [P, HALVES, SEQ, HEADS])
        sc_sum = sb("sc_sum", [P, HALVES, SEQ, HEADS])
        sc_inv = sb("sc_inv", [P, HALVES, SEQ, HEADS])
        attT = z1_sb[:, :, :].rearrange("p n i -> p (n i)").rearrange("p (c t) -> p c t", c=KC)
        stats = sb("stats", [P, 3, NT, 6])
        mv = sb("mv", [P, 3, NT, 2])
        veps = sb("veps", [P, 3, NT])
        rstd = sb("rstd", [P, 3, NT])
        neg_half = sb("neg_half", [P, NT])
        negmax = sb("negmax", [P, SEQ * CTXT])
        xa_sum = sb("xa_sum", [P, SEQ * CTXT])
        xa_inv = sb("xa_inv", [P, SEQ * CTXT])
        xa_T = qkT[:, :, :].rearrange("p a n -> p (a n)").rearrange(
            "p (s c m) -> p s c m", s=SEQ, c=CTXT)
        xa_exp = sb("xa_exp", [P, SEQ * CTXT, SEQ * 64])
        xa_prob = xa_exp
        idx_sb = sb("idx_sb", [P, FT], I32)
        wgu_sb = sb("wgu_sb", [P, 2, FT, HID])
        wd_sb = sb("wd_sb", [P, KC, FF])
        w_max = sb("w_max", [P, 2 * FT + KC])
        w_scale = sb("w_scale", [P, 2 * FT + KC])
        w_inv = sb("w_inv", [P, 2 * FT + KC])
        w_big = sb("w_big", [P, 2, FT * HID])
        qgu = sb("qgu", [P, 2, FT * HID], BF16)
        qwd = sb("qwd", [P, KC, FPAD], BF16)
        qguT = sb("qguT", [P, KC, 2, FF], BF16)
        qwdT = sb("qwdT", [P, FT, HID], BF16)
        diag = sb("diag", [P, 2 * FT + KC, P])
        wsb_gu = sb("wsb_gu", [P, 2, FF])
        wsb_d = sb("wsb_d", [P, HID])
        z_max = sb("z_max", [P, NT])
        z_scale = sb("z_scale", [P, NT])
        z_inv = sb("z_inv", [P, NT])
        z_val = z3_sb
        z_big = z2_sb
        qx = sb("qx", [P, NT, HID], BF16)
        qxT = sb("qxT", [P, NT, KC, P], BF16)
        t_sb = sb("t_sb", [P, 2, FF])
        t_max = sb("t_max", [P, NT])
        t_scale = sb("t_scale", [P, NT])
        t_inv = sb("t_inv", [P, NT])
        o_scale = sb("o_scale", [P, NT])
        t_val = t_sb
        qt = sb("qt", [P, 2, FPAD], BF16)
        qtT = sb("qtT", [P, 2, FT, P], BF16)
        o1 = sb("o1", [P, 2, HID])
        wproj_ord = o1
        y_sb = x_sb
        ident = sb("ident", [P, P])
        identb = sb("identb", [P, P], BF16)
        ones = sb("ones", [P, P])

        bank = [es.enter_context(nc.psum_tensor(f"bank{i}", [P, 512], F32)) for i in range(8)]
        FFN_BANKS = [(0, 1), (4, 5), (2, 3)]
        QT_BANK, DOWN_BANK = 6, 7

        x_in = [sem(f"x_in{h}") for h in range(HALVES)]
        wqkv_in, wproj_in, wx_in, ctx_in, idx_in, wd_in, wgu_in, out_written = (
            sem(n) for n in ("wqkv_in", "wproj_in", "wx_in", "ctx_in", "idx_in", "wd_in",
                             "wgu_in", "out_written"))
        wproj_ordered = sem("wproj_ordered")
        gp_step, consts_ready, tails_ready, rstd_ready, diag_ready, probs_x_ready, y_ready = (
            sem(n) for n in ("gp_step", "consts_ready", "tails_ready", "rstd_ready",
                             "diag_ready", "probs_x_ready", "y_ready"))
        (wT_ps, ctxT_ps, z1T_ps, qkT_ps, qkv_ps, energy_ps, wsb_ps, qwT_ps, attT_ps, proj_ps,
         z2T_ps, xm_ps, probsT_ps, qxT_ps, ffn_ps, qtT_ps, down_ps) = (
            sem(n) for n in ("wT_ps", "ctxT_ps", "z1T_ps", "qkT_ps", "qkv_ps", "energy_ps",
                             "wsb_ps", "qwT_ps", "attT_ps", "proj_ps", "z2T_ps", "xm_ps", "probsT_ps",
                             "qxT_ps", "ffn_ps", "qtT_ps", "down_ps"))
        (wT_out, ctxT_out, z1T_out, qkT_out, kv_out, xexp_done, exp_done, wsb_out, w_val_ready,
         w_big_ready, qwT_out, attT_out, z2T_out, z_val_ready, z_big_ready, qxT_out, silu_done,
         t_val_ready, t_big_ready, qtT_out, probsT_out) = (
            sem(n) for n in ("wT_out", "ctxT_out", "z1T_out", "qkT_out", "kv_out", "xexp_done",
                             "exp_done", "wsb_out", "w_val_ready", "w_big_ready", "qwT_out",
                             "attT_out", "z2T_out", "z_val_ready", "z_big_ready", "qxT_out",
                             "silu_done", "t_val_ready", "t_big_ready", "qtT_out", "probsT_out"))
        (dve_step, stats_ready, z1_ready, negmax_ready, q_used, centred, pv_ready, xa_inv_ready,
         w_scale_ready, w_round, x1_ready, z2_ready, x2_ready, z3_ready, z_inv_ready, qx_ready,
         g1_ready, u1_ready, t_ready, t_inv_ready, qt_ready, o1_ready) = (
            sem(n) for n in ("dve_step", "stats_ready", "z1_ready", "negmax_ready", "q_used",
                             "centred", "pv_ready", "xa_inv_ready", "w_scale_ready", "w_round",
                             "x1_ready", "z2_ready", "x2_ready", "z3_ready", "z_inv_ready",
                             "qx_ready", "g1_ready", "u1_ready", "t_ready", "t_inv_ready",
                             "qt_ready", "o1_ready"))

        block = es.enter_context(nc.Block())

        @block.sync
        def _(sp):
            rows = w_qkv.rearrange("(g r d) i -> r g d i", g=KVH, r=QPK + 2)
            for h in range(HALVES):
                sp.dma_start(x_sb[:, h * SEQ:(h + 1) * SEQ, :],
                             x[:, h * P:(h + 1) * P, :].rearrange("s p i -> p s i")).then_inc(x_in[h], 16)
            for r in range(QPK + 2):
                sp.dma_start(wqkv_sb[(r % 2) * KVD:(r % 2 + 1) * KVD, r // 2, :], rows[r]).then_inc(wqkv_in, 16)
            sp.dma_start(wproj_sb[:, :, :], w_proj.rearrange("(t p) i -> p t i", p=P)).then_inc(wproj_in, 16)
            sp.dma_start(wd_sb[:, :, :], w_down.rearrange("(t p) i -> p t i", p=P)).then_inc(wd_in, 16)
            for n in range(NT):
                h, s = n // SEQ, n % SEQ
                sp.wait_ge(y_ready, n + 1)
                sp.dma_start(out[s, h * P:(h + 1) * P, :], y_sb[:, n, :]).then_inc(out_written, 16)
            sp.wait_ge(out_written, 16 * NT)

        @block.gpsimd
        def _(gp):
            gp.memset(wgu_sb[:, :, FT - 1, :], 1.0).then_inc(gp_step, 1)
            gp.memset(ident[:, :], 0.0).then_inc(gp_step, 1)
            gp.memset(identb[:, :], 0.0).then_inc(gp_step, 1)
            gp.memset(ones[:, :], 1.0).then_inc(consts_ready, 1)
            gp.memset(neg_half[:, :], -0.5).then_inc(consts_ready, 1)
            gp.wait_ge(gp_step, 3)
            gp.affine_select(out=ident[:, :], in_=ident[:, :], compare_op=ALU.not_equal, fill=1.0,
                             base=0, pattern=[[-1, P]], channel_multiplier=1).then_inc(consts_ready, 1)
            gp.affine_select(out=identb[:, :], in_=identb[:, :], compare_op=ALU.not_equal, fill=1.0,
                             base=0, pattern=[[-1, P]], channel_multiplier=1).then_inc(consts_ready, 1)
            gp.wait_ge(idx_in, 32)
            for t in range(FT):
                rows = P if t < FT - 1 else FLAST
                for a, w in enumerate((w_gate, w_up)):
                    gp.indirect_dma_start(
                        wgu_sb[0:rows, a, t, :], None, w,
                        bass.IndirectOffsetOnAxis(ap=idx_sb[0:rows, t:t + 1], axis=0),
                    ).then_inc(wgu_in, 16)
            gp.wait_ge(wproj_in, 16)
            for t in range(KC):
                gp.tensor_copy(wproj_ord[:, t, :].rearrange("p (h g d) -> p h g d", g=KVH, h=QPK),
                               wproj_sb[:, t, :].rearrange("p (g h d) -> p h g d", g=KVH, h=QPK)
                               ).then_inc(wproj_ordered, 1)
            gp.memset(sc[:, :, :, :, :], -3.0e38).then_inc(tails_ready, 1)
            gp.memset(qwd[:, :, FF:FPAD], 0.0).then_inc(tails_ready, 1)
            gp.memset(qt[:, :, FF:FPAD], 0.0).then_inc(tails_ready, 1)

            pows = [0]

            def inverse_deviation(ln, h):
                pows[0] += 1
                sl = slice(h * SEQ, (h + 1) * SEQ)
                gp.wait_ge(stats_ready, pows[0])
                gp.tensor_scalar(veps[:, ln, sl], mv[:, ln, sl, 1], EPS, 1.0, ALU.add, ALU.mult).then_inc(gp_step, 1)
                gp.wait_ge(gp_step, 3 + pows[0])
                gp.tensor_tensor(rstd[:, ln, sl], veps[:, ln, sl], neg_half[:, 0:SEQ], ALU.pow).then_inc(rstd_ready, 1)

            inverse_deviation(0, 0)
            inverse_deviation(0, 1)
            for s in range(SEQ):
                gp.wait_ge(xa_inv_ready, s + 1)
                for t in range(CTXT):
                    i = s * CTXT + t
                    gp.tensor_scalar(xa_prob[:, i, :], xa_exp[:, i, :], xa_inv[:, i:i + 1], 1.0,
                                     ALU.mult, ALU.mult).then_inc(probs_x_ready, 1)
            gp.wait_ge(w_scale_ready, 1)
            for i in range(2 * FT + KC):
                gp.tensor_scalar(diag[:, i, :], ident[:, :], w_scale[:, i:i + 1], 1.0,
                                 ALU.mult, ALU.mult).then_inc(diag_ready, 1)
            for ln in (1, 2):
                for h in range(HALVES):
                    inverse_deviation(ln, h)
            for n in range(NT):
                gp.wait_ge(o1_ready, n + 1)
                gp.tensor_tensor(y_sb[:, n, :], o1[:, n % 2, :], x2_sb[:, n, :], ALU.add).then_inc(y_ready, 1)

        @block.tensor
        def _(pe):
            def transpose(dst, src, idn=ident):
                return pe.transpose(dst, src, idn)

            pe.wait_ge(consts_ready, 4)
            pe.wait_ge(wqkv_in, 16 * (QPK + 2))
            for c in range(KC):
                for r in range(QKV // P):
                    last = transpose(bank[4 + c][:, r * P:(r + 1) * P], wqkv_sb[:, r, c * P:(c + 1) * P], ident[:, :])
                last.then_inc(wT_ps, 1)
            pe.wait_ge(ctx_in, 16)
            for u in range(2):
                for j in range(4):
                    last = transpose(bank[6 + u][:, j * P:(j + 1) * P], ctx_sb[:, 4 * u + j, :], ident[:, :])
                last.then_inc(ctxT_ps, 1)
            pe.wait_ge(wx_in, 64)
            for a in range(2):
                last = transpose(bank[0][:, a * P:(a + 1) * P], wx_sb[:, a, :], ident[:, :])
            last.then_inc(wT_ps, 1)
            pe.wait_ge(wproj_ordered, KC)
            for c in range(KC):
                for t in range(KC):
                    last = transpose(bank[1][:, c * HID + t * P:c * HID + (t + 1) * P],
                                     wproj_ord[:, t, c * P:(c + 1) * P], ident[:, :])
            last.then_inc(wT_ps, 1)

            def norm_T(h, banks, src, done):
                for u in range(2):
                    b = bank[banks[u]]
                    for c in range(KC):
                        for j in range(2):
                            n = h * SEQ + 2 * u + j
                            last = transpose(b[:, (2 * c + j) * P:(2 * c + j + 1) * P],
                                             src[:, n, c * P:(c + 1) * P], ident[:, :])
                    last.then_inc(done, 1)

            def qkv(h):
                for s in range(SEQ):
                    n = h * SEQ + s
                    pe.wait_ge(z1T_out, 2 * h + s // 2 + 1)
                    if h == 0:
                        pe.wait_ge(wT_out, 3 if s == 0 else 4)
                        if s >= 2:
                            pe.wait_ge(z1T_out, 2)
                    else:
                        pe.wait_ge(q_used, s + 1)
                        pe.wait_ge(kv_out, s + 1)
                    for c in range(KC):
                        last = pe.matmul(bank[s][:, 0:QKV], z1T[:, c, n * P:(n + 1) * P], wqkvT[:, c, :],
                                         start=(c == 0), stop=(c == KC - 1))
                    last.then_inc(qkv_ps, 1)

            pe.wait_ge(z1_ready, SEQ)
            norm_T(0, (2, 3), z1_sb, z1T_ps)
            pe.wait_ge(wT_out, 3)
            for u in range(2):
                pe.wait_ge(ctxT_out, u + 1)
                if u == 1:
                    pe.wait_ge(ctxT_out, 2)
                else:
                    pe.wait_ge(wT_out, 2)
                for a in range(2):
                    pe.matmul(bank[4 + 2 * u + a][:, :], wxT[:, a, :], ctxT[:, u * 512:(u + 1) * 512],
                              start=True, stop=True).then_inc(qkT_ps, 1)
            qkv(0)
            for s in range(SEQ):
                pe.wait_ge(qkT_out, 2 if s < 2 else 4)
                for t in range(CTXT):
                    last = pe.matmul(bank[4 + s][:, t * 256:(t + 1) * 256],
                                     qkT[:, 0, (s * CTXT + t) * P:(s * CTXT + t + 1) * P],
                                     qkT[:, 1, s * 256:(s + 1) * 256], start=True, stop=True)
                last.then_inc(energy_ps, 1)
            pe.wait_ge(z1_ready, 2 * SEQ)
            pe.wait_ge(xexp_done, 4)
            norm_T(1, (4, 5), z1_sb, z1T_ps)
            qkv(1)
            pe.wait_ge(xexp_done, 8)
            pe.wait_ge(diag_ready, 2 * FT + KC)
            for a in range(2):
                for t in range(4):
                    last = pe.matmul(bank[6 + a][:, t * P:(t + 1) * P], ones[:, :], diag[:, a * FT + t, :],
                                     start=True, stop=True)
                last.then_inc(wsb_ps, 1)
            pe.wait_ge(z1T_out, 4)
            for a in range(2):
                at = a * (FF - 512)
                pe.matmul(bank[4][:, at:at + P], ones[:, :], diag[:, a * FT + 4, :], start=True, stop=True)
                last = pe.matmul(bank[4][:, at + P:at + P + FLAST], ones[0:FLAST, :],
                                 diag[0:FLAST, a * FT + 5, 0:FLAST], start=True, stop=True)
            last.then_inc(wsb_ps, 1)
            for t in range(KC):
                last = pe.matmul(bank[5][:, t * P:(t + 1) * P], ones[:, :], diag[:, 2 * FT + t, :],
                                 start=True, stop=True)
            last.then_inc(wsb_ps, 1)

            def attention_T(h, banks):
                for u in range(2):
                    for c in range(KC):
                        for j in range(2):
                            q = 2 * u + j
                            if c == 0:
                                pe.wait_ge(pv_ready, h * SEQ + q + 1)
                            for k in range(q + 1):
                                last = pe.matmul(bank[banks[u]][:, (2 * c + j) * P:(2 * c + j + 1) * P],
                                                 pv[:, h, first_pair[q] + k, c * P:(c + 1) * P],
                                                 ident[:, :], start=(k == 0), stop=(k == q))
                    last.then_inc(attT_ps, 1)

            def project(h, banks):
                for u in range(2):
                    pe.wait_ge(attT_out, 2 * h + u + 1)
                    for j in range(2):
                        n = h * SEQ + 2 * u + j
                        for c in range(KC):
                            last = pe.matmul(bank[banks[u]][:, j * HID:(j + 1) * HID],
                                             attT[:, c, n * P:(n + 1) * P], wprojT[:, c, :],
                                             start=(c == 0), stop=(c == KC - 1))
                    last.then_inc(proj_ps, 1)

            def mix(h, banks):
                for u in range(2):
                    pe.wait_ge(z2T_out, 2 * h + u + 1)
                    for j in range(2):
                        s = 2 * u + j
                        n = h * SEQ + s
                        for c in range(KC):
                            last = pe.matmul(bank[banks[u]][:, j * HID:(j + 1) * HID],
                                             z2T[:, c, n * P:(n + 1) * P], xa_T[:, s, c, :],
                                             start=(c == 0), stop=(c == KC - 1))
                    last.then_inc(xm_ps, 1)

            def weights_T(a):
                pe.wait_ge(w_round, a + 1)
                for c in range(KC):
                    b = bank[4 + 2 * a + c][:, :].bitcast(BF16)
                    for t in range(FT):
                        rows = P if t < FT - 1 else FLAST
                        last = transpose(b[:, t * P:t * P + rows],
                                         qgu[0:rows, a, t * HID + c * P:t * HID + (c + 1) * P],
                                         identb[0:rows, 0:rows])
                    last.then_inc(qwT_ps, 1)

            pe.wait_ge(wsb_out, 4)
            for s in range(SEQ):
                pe.wait_ge(probs_x_ready, (s + 1) * CTXT)
                for c in range(CTXT):
                    for t in range(CTXT):
                        last = transpose(bank[4 + s][:, (c * CTXT + t) * P:(c * CTXT + t + 1) * P],
                                         xa_prob[:, s * CTXT + t, c * P:(c + 1) * P], ident[:, :])
                last.then_inc(probsT_ps, 1)
            pe.wait_ge(probsT_out, 2)
            attention_T(0, (4, 5))
            pe.wait_ge(probsT_out, 4)
            project(0, (6, 7))
            pe.wait_ge(q_used, 2 * SEQ)
            pe.wait_ge(kv_out, 2 * SEQ)
            attention_T(1, (0, 1))
            project(1, (2, 3))
            pe.wait_ge(attT_out, 2)
            weights_T(0)
            pe.wait_ge(x1_ready, 2)
            weights_T(1)
            pe.wait_ge(w_round, 3)
            for u in range(2):
                pe.wait_ge(qwT_out, 1 + u)
                b = bank[4 + u][:, :].bitcast(BF16)
                for j in range(3):
                    for t in range(KC):
                        last = transpose(b[:, j * HID + t * P:j * HID + (t + 1) * P],
                                         qwd[:, t, (3 * u + j) * P:(3 * u + j + 1) * P], identb[:, :])
                last.then_inc(qwT_ps, 1)
            pe.wait_ge(qwT_out, 6)
            pe.wait_ge(z2_ready, SEQ)
            norm_T(0, (4, 5), z2_sb, z2T_ps)
            mix(0, (6, 7))
            pe.wait_ge(z2_ready, 2 * SEQ)
            pe.wait_ge(attT_out, 4)
            norm_T(1, (0, 1), z2_sb, z2T_ps)
            pe.wait_ge(x1_ready, 4)
            mix(1, (2, 3))

            def rounded_T(h, b):
                pe.wait_ge(qx_ready, h + 1)
                bb = bank[b][:, :].bitcast(BF16)
                for j in range(SEQ):
                    for c in range(KC):
                        k = j * KC + c
                        last = transpose(bb[:, k * P:(k + 1) * P],
                                         qx[:, h * SEQ + j, c * P:(c + 1) * P], identb[:, :])
                last.then_inc(qxT_ps, 1)

            pe.wait_ge(x2_ready, 2)
            rounded_T(0, QT_BANK)

            def gate_up(n):
                for k in range(2):
                    i = 2 * n + k
                    if i >= 3:
                        pe.wait_ge(g1_ready, i - 2)
                        pe.wait_ge(u1_ready, i - 2)
                    for a in range(2):
                        for c in range(KC):
                            last = pe.matmul(bank[FFN_BANKS[i % 3][a]][:, 0:FH], qxT[:, n, c, :],
                                             qguT[:, c, a, k * FH:(k + 1) * FH],
                                             start=(c == 0), stop=(c == KC - 1))
                    last.then_inc(ffn_ps, 1)

            def down(n):
                pe.wait_ge(qt_ready, n + 1)
                if n >= 1:
                    pe.wait_ge(qtT_out, n)
                bb = bank[QT_BANK][:, :].bitcast(BF16)
                for t in range(FT):
                    last = transpose(bb[:, t * P:(t + 1) * P], qt[:, n % 2, t * P:(t + 1) * P], identb[:, :])
                last.then_inc(qtT_ps, 1)
                pe.wait_ge(qtT_out, n + 1)
                if n >= 1:
                    pe.wait_ge(o1_ready, n)
                for t in range(FT):
                    last = pe.matmul(bank[DOWN_BANK][:, 0:HID], qtT[:, n % 2, t, :], qwdT[:, t, :],
                                     start=(t == 0), stop=(t == FT - 1))
                last.then_inc(down_ps, 1)

            pe.wait_ge(z2T_out, 4)
            for n in range(NT):
                if n == 0:
                    pe.wait_ge(qxT_out, 1)
                if n == 1:
                    pe.wait_ge(x2_ready, 4)
                    rounded_T(1, DOWN_BANK)
                    pe.wait_ge(qxT_out, 2)
                gate_up(n)
                if n >= 2:
                    down(n - 2)
            down(NT - 2)
            down(NT - 1)

        @block.scalar
        def _(act):
            if down_index.dtype == mybir.dt.int64:
                low = down_index.bitcast(I32).rearrange("(j w) -> j w", w=2)[:, 0:1]
            else:
                low = down_index.rearrange("(j w) -> j w", w=1)
            act.dma_start(idx_sb[:, 0:FT - 1],
                          low[0:(FT - 1) * P].rearrange("(t p) w -> p (t w)", p=P),
                          allow_slow_non_contiguous=True).then_inc(idx_in, 16)
            act.dma_start(idx_sb[0:FLAST, FT - 1:FT], low[(FT - 1) * P:FF]).then_inc(idx_in, 16)
            act.dma_start(ctx_sb[:, :, :], ctx_feat.rearrange("s (t p) c -> p (s t) c", p=P)).then_inc(ctx_in, 16)
            act.dma_start(wx_sb[:, 0, :], w_q).then_inc(wx_in, 16)
            act.dma_start(wx_sb[:, 1, :], w_k).then_inc(wx_in, 16)
            act.dma_start(bx_sb[:, 0:1], b_q.rearrange("(p w) -> p w", w=1)).then_inc(wx_in, 16)
            act.dma_start(bx_sb[:, 1:2], b_k.rearrange("(p w) -> p w", w=1)).then_inc(wx_in, 16)

            def copy(dst, src, scale=1.0):
                return act.activation(dst, src, ACT.Copy, scale=scale)

            for c in range(KC):
                act.wait_ge(wT_ps, c + 1)
                copy(wqkvT[:, c, :], bank[4 + c][:, 0:QKV]).then_inc(wT_out, 1)
            for u in range(2):
                act.wait_ge(ctxT_ps, u + 1)
                copy(ctxT[:, u * 512:(u + 1) * 512], bank[6 + u][:, :]).then_inc(ctxT_out, 1)
            act.wait_ge(wT_ps, 3)
            copy(wxT[:, :, :], bank[0][:, 0:2 * P].rearrange("p (a c) -> p a c", a=2)).then_inc(wT_out, 1)
            act.wait_ge(wT_ps, 4)
            copy(wprojT[:, :, :], bank[1][:, :].rearrange("p (a c) -> p a c", a=KC)).then_inc(wT_out, 1)

            def half_T(dst, h, banks, full, done):
                for u in range(2):
                    act.wait_ge(full, 2 * h + u + 1)
                    n = h * SEQ + 2 * u
                    copy(dst[:, :, n * P:(n + 2) * P],
                         bank[banks[u]][:, :].rearrange("p (c t) -> p c t", c=KC)).then_inc(done, 1)

            def keys_values(h):
                for s in range(SEQ):
                    act.wait_ge(qkv_ps, h * SEQ + s + 1)
                    copy(kv_sb[:, h * SEQ + s, :], bank[s][:, HID:QKV]).then_inc(kv_out, 1)

            def exp_scores(h):
                act.wait_ge(centred, h + 1)
                act.activation(e_sb[:, h], sc[:, h], ACT.Exp, scale=SCALE).then_inc(exp_done, 1)

            half_T(z1T, 0, (2, 3), z1T_ps, z1T_out)
            for u in range(2):
                for a in range(2):
                    act.wait_ge(qkT_ps, 2 * u + a + 1)
                    act.activation(qkT[:, a, u * 512:(u + 1) * 512], bank[4 + 2 * u + a][:, :],
                                   ACT.Identity, bias=bx_sb[:, a:a + 1], scale=1.0).then_inc(qkT_out, 1)
            keys_values(0)
            for s in range(SEQ):
                act.wait_ge(negmax_ready, s + 1)
                for t in range(CTXT):
                    i = s * CTXT + t
                    act.activation(xa_exp[:, i, :], bank[4 + s][:, t * 256:(t + 1) * 256], ACT.Exp,
                                   bias=negmax[:, i:i + 1], accum_out=xa_sum[:, i:i + 1]).then_inc(xexp_done, 1)
            half_T(z1T, 1, (4, 5), z1T_ps, z1T_out)
            exp_scores(0)
            keys_values(1)

            def over_scale(a):
                act.wait_ge(w_scale_ready, 1)
                tiles, width = (FT, HID) if a < 2 else (KC, FF)
                for t in range(tiles):
                    src = wgu_sb[:, a, t, :] if a < 2 else wd_sb[:, t, :]
                    i = a * FT + t
                    copy(src, src, scale=w_inv[:, i:i + 1]).then_inc(w_val_ready, 1)
                act.wait_ge(w_val_ready, (FT, 2 * FT, 2 * FT + KC)[a])
                src = wgu_sb[:, a] if a < 2 else wd_sb[:, :, :]
                if a == 2:
                    act.wait_ge(w_round, 1)
                copy(w_big[:, a % 2, 0:tiles * width].rearrange("p (t i) -> p t i", t=tiles), src,
                     scale=SHIFT).then_inc(w_big_ready, 1)

            over_scale(0)
            exp_scores(1)
            over_scale(1)
            for a in range(2):
                act.wait_ge(wsb_ps, a + 1)
                copy(wsb_gu[:, a, 0:512], bank[6 + a][:, :]).then_inc(wsb_out, 1)
            act.wait_ge(wsb_ps, 3)
            copy(wsb_gu[:, :, 512:FF],
                 bank[4][:, 0:2 * (FF - 512)].rearrange("p (a c) -> p a c", a=2)).then_inc(wsb_out, 1)
            act.wait_ge(wsb_ps, 4)
            copy(wsb_d[:, :], bank[5][:, 0:HID]).then_inc(wsb_out, 1)
            for s in range(SEQ):
                act.wait_ge(probsT_ps, s + 1)
                copy(xa_T[:, s, :, :],
                     bank[4 + s][:, :].rearrange("p (c m) -> p c m", c=CTXT)).then_inc(probsT_out, 1)
            half_T(attT, 0, (4, 5), attT_ps, attT_out)
            over_scale(2)
            half_T(attT, 1, (0, 1), attT_ps, attT_out)
            for a in range(2):
                for c in range(KC):
                    act.wait_ge(qwT_ps, 2 * a + c + 1)
                    copy(qguT[:, c, a, :], bank[4 + 2 * a + c][:, :].bitcast(BF16)[:, 0:FF]).then_inc(qwT_out, 1)
            for u in range(2):
                act.wait_ge(qwT_ps, 5 + u)
                copy(qwdT[:, 3 * u:3 * u + 3, :],
                     bank[4 + u][:, :].bitcast(BF16)[:, 0:3 * HID].rearrange("p (t o) -> p t o", t=3)
                     ).then_inc(qwT_out, 1)
            half_T(z2T, 0, (4, 5), z2T_ps, z2T_out)
            half_T(z2T, 1, (0, 1), z2T_ps, z2T_out)

            def z_over_scale(h):
                act.wait_ge(z_inv_ready, h + 1)
                for s in range(SEQ):
                    n = h * SEQ + s
                    copy(z_val[:, n, :], z3_sb[:, n, :], scale=z_inv[:, n:n + 1]).then_inc(z_val_ready, 1)
                act.wait_ge(z_val_ready, (h + 1) * SEQ)
                copy(z_big[:, h * SEQ:(h + 1) * SEQ, :], z_val[:, h * SEQ:(h + 1) * SEQ, :],
                     scale=SHIFT).then_inc(z_big_ready, 1)

            def z_T(h, b):
                act.wait_ge(qxT_ps, h + 1)
                copy(qxT[:, h * SEQ:(h + 1) * SEQ, :, :],
                     bank[b][:, :].bitcast(BF16).rearrange("p (n c t) -> p n c t", n=SEQ, c=KC)
                     ).then_inc(qxT_out, 1)

            z_over_scale(0)
            z_over_scale(1)
            z_T(0, QT_BANK)
            z_T(1, DOWN_BANK)

            def silu(n):
                for k in range(2):
                    act.wait_ge(g1_ready, 2 * n + k + 1)
                    if n >= 2:
                        act.wait_ge(t_ready, 2 * (n - 2) + k + 1)
                    act.activation(sg[:, n % 2, k * FH:(k + 1) * FH], g1[:, n % 2, k * FH:(k + 1) * FH],
                                   ACT.Silu, scale=z_scale[:, n:n + 1]).then_inc(silu_done, 1)

            def t_over_scale(n):
                act.wait_ge(t_inv_ready, n + 1)
                if n >= 2:
                    act.wait_ge(qt_ready, n - 1)
                copy(t_val[:, n % 2, :], t_sb[:, n % 2, :], scale=t_inv[:, n:n + 1]).then_inc(t_val_ready, 1)
                act.wait_ge(t_val_ready, n + 1)
                copy(t_big[:, n % 2, :], t_val[:, n % 2, :], scale=SHIFT).then_inc(t_big_ready, 1)

            def t_T(n):
                act.wait_ge(qtT_ps, n + 1)
                if n >= 2:
                    act.wait_ge(down_ps, n - 1)
                copy(qtT[:, n % 2, :, :],
                     bank[QT_BANK][:, :].bitcast(BF16)[:, 0:FPAD].rearrange("p (k t) -> p k t", k=FT)
                     ).then_inc(qtT_out, 1)

            for n in range(NT + 2):
                if n < NT:
                    silu(n)
                if n >= 2:
                    t_T(n - 2)
                if n < NT:
                    t_over_scale(n)

        @block.vector
        def _(dve):
            v = nc.vector
            steps = [0]

            def step(ins):
                steps[0] += 1
                ins.then_inc(dve_step, 1)
                dve.wait_ge(dve_step, steps[0])

            bn = [0]

            def statistics(ln, src, h):
                for n in range(h * SEQ, (h + 1) * SEQ):
                    last = v.bn_stats(stats[:, ln, n, :], src[:, n, :])
                step(last)
                for n in range(h * SEQ, (h + 1) * SEQ):
                    last = v.bn_aggr(mv[:, ln, n, :], stats[:, ln, n, :])
                last.then_inc(stats_ready, 1)
                bn[0] += 1

            def normalise(ln, src, dst, h, ready, nth):
                dve.wait_ge(rstd_ready, nth)
                for n in range(h * SEQ, (h + 1) * SEQ):
                    v.tensor_scalar(dst[:, n, :], src[:, n, :], mv[:, ln, n, 0:1], rstd[:, ln, n:n + 1],
                                    ALU.subtract, ALU.mult).then_inc(ready, 1)

            for h in range(HALVES):
                dve.wait_ge(x_in[h], 16)
                statistics(0, x_sb, h)
            normalise(0, x_sb, z1_sb, 0, z1_ready, 1)
            normalise(0, x_sb, z1_sb, 1, z1_ready, 2)

            def query_key(h):
                dve.wait_ge(tails_ready, 3)
                for q in range(SEQ):
                    nk = q + 1
                    dve.wait_ge(kv_out, h * SEQ + q + 1)
                    pr = prod[:, first_pair[q]:first_pair[q] + nk, :]
                    v.tensor_tensor(
                        pr.rearrange("p k (h e) -> p k h e", h=QPK),
                        bank[q][:, 0:HID].rearrange("p (h e) -> p h e", h=QPK).unsqueeze(1).broadcast_to([P, nk, QPK, KVD]),
                        kv_sb[:, h * SEQ:h * SEQ + nk, 0:KVD].unsqueeze(2).broadcast_to([P, nk, QPK, KVD]),
                        ALU.mult).then_inc(q_used, 1)
                for q in range(SEQ):
                    nk = q + 1
                    if q == 0:
                        dve.wait_ge(q_used, (h + 1) * SEQ)
                    pr = prod[:, first_pair[q]:first_pair[q] + nk, :]
                    last = v.tensor_reduce(sc[:, h, q, 0:nk, :], pr.rearrange("p k (c d) -> p k c d", d=HD),
                                           AX.X, ALU.add)
                step(last)
                step(v.tensor_reduce(sc_max[:, h], sc[:, h].rearrange("p q k c -> p q c k"), AX.X, ALU.max))
                v.tensor_tensor(sc[:, h], sc[:, h],
                                sc_max[:, h].unsqueeze(2).broadcast_to([P, SEQ, SEQ, HEADS]),
                                ALU.subtract).then_inc(centred, 1)

            def weighted_values(h):
                dve.wait_ge(exp_done, h + 1)
                step(v.tensor_reduce(sc_sum[:, h], e_sb[:, h].rearrange("p q k c -> p q c k"), AX.X, ALU.add))
                step(v.reciprocal(sc_inv[:, h], sc_sum[:, h]))
                step(v.tensor_tensor(e_sb[:, h], e_sb[:, h],
                                     sc_inv[:, h].unsqueeze(2).broadcast_to([P, SEQ, SEQ, HEADS]), ALU.mult))
                for q in range(SEQ):
                    nk = q + 1
                    full = [P, nk, QPK, KVH, HD]
                    v.tensor_tensor(
                        pv[:, h, first_pair[q]:first_pair[q] + nk, :].rearrange("p k (h g d) -> p k h g d", h=QPK, g=KVH),
                        e_sb[:, h, q, 0:nk, :].rearrange("p k (h g) -> p k h g", h=QPK).unsqueeze(4).broadcast_to(full),
                        kv_sb[:, h * SEQ:h * SEQ + nk, KVD:2 * KVD].rearrange("p k (g d) -> p k g d", g=KVH)
                        .unsqueeze(2).broadcast_to(full),
                        ALU.mult).then_inc(pv_ready, 1)

            def negate_maxima():
                for s in range(SEQ):
                    dve.wait_ge(energy_ps, s + 1)
                    v.tensor_reduce(negmax[:, s * CTXT:(s + 1) * CTXT],
                                    bank[4 + s][:, :].rearrange("p (t m) -> p t m", t=CTXT),
                                    AX.X, ALU.max, negate=True).then_inc(negmax_ready, 1)

            def context_sums():
                for s in range(SEQ):
                    dve.wait_ge(xexp_done, (s + 1) * CTXT)
                    v.reciprocal(xa_inv[:, s * CTXT:(s + 1) * CTXT],
                                 xa_sum[:, s * CTXT:(s + 1) * CTXT]).then_inc(xa_inv_ready, 1)

            def weight_scales():
                dve.wait_ge(wgu_in, 16 * 2 * FT)
                dve.wait_ge(wd_in, 16)
                v.tensor_reduce(w_max[:, 0:2 * FT], wgu_sb[:, :, :, :].rearrange("p a t i -> p (a t) i"),
                                AX.X, ALU.max, apply_absolute_value=True)
                step(v.tensor_reduce(w_max[:, 2 * FT:], wd_sb[:, :, :], AX.X, ALU.max,
                                     apply_absolute_value=True))
                step(v.tensor_scalar(w_scale[:, :], w_max[:, :], 1.0 / FP8_MAX, None, ALU.mult))
                v.reciprocal(w_inv[:, :], w_scale[:, :]).then_inc(w_scale_ready, 1)

            def round_fp8(dst, val, big, ready):
                step(v.tensor_scalar(big.bitcast(I32), big.bitcast(I32), EXP_BITS, HALF_BIT,
                                     ALU.bitwise_and, ALU.bitwise_or))
                step(v.scalar_tensor_tensor(val, big, M_LEAST, val, ALU.max, ALU.add))
                v.scalar_tensor_tensor(dst, big, M_LEAST, val, ALU.max, ALU.subtract).then_inc(ready, 1)

            def round_weights(a):
                dve.wait_ge(w_big_ready, a + 1)
                if a < 2:
                    round_fp8(qgu[:, a, :], wgu_sb[:, a].rearrange("p t i -> p (t i)"), w_big[:, a, :], w_round)
                else:
                    w = KC * FF
                    round_fp8(qwd[:, :, 0:FF], wd_sb[:, :, :],
                              w_big[:, 0, 0:w].rearrange("p (t i) -> p t i", t=KC), w_round)

            def add_residual(h, base, banks, dst, full, ready):
                for u in range(2):
                    dve.wait_ge(full, 2 * h + u + 1)
                    n = h * SEQ + 2 * u
                    v.tensor_tensor(dst[:, n:n + 2, :],
                                    bank[banks[u]][:, :].rearrange("p (j i) -> p j i", j=2),
                                    base[:, n:n + 2, :], ALU.add).then_inc(ready, 1)
                dve.wait_ge(ready, 2 * h + 2)

            def z_scales(h):
                sl = slice(h * SEQ, (h + 1) * SEQ)
                dve.wait_ge(z3_ready, (h + 1) * SEQ)
                step(v.tensor_reduce(z_max[:, sl], z3_sb[:, sl, :], AX.X, ALU.max, apply_absolute_value=True))
                step(v.tensor_scalar(z_scale[:, sl], z_max[:, sl], 1.0 / FP8_MAX, None, ALU.mult))
                v.reciprocal(z_inv[:, sl], z_scale[:, sl]).then_inc(z_inv_ready, 1)

            def round_z(h):
                sl = slice(h * SEQ, (h + 1) * SEQ)
                dve.wait_ge(z_big_ready, h + 1)
                round_fp8(qx[:, sl, :], z_val[:, sl, :], z_big[:, sl, :], qx_ready)

            negate_maxima()
            query_key(0)
            context_sums()
            weighted_values(0)
            weight_scales()
            query_key(1)
            round_weights(0)
            weighted_values(1)
            round_weights(1)
            add_residual(0, x_sb, (6, 7), x1_sb, proj_ps, x1_ready)
            statistics(1, x1_sb, 0)
            add_residual(1, x_sb, (2, 3), x1_sb, proj_ps, x1_ready)
            statistics(1, x1_sb, 1)
            normalise(1, x1_sb, z2_sb, 0, z2_ready, 3)
            normalise(1, x1_sb, z2_sb, 1, z2_ready, 4)
            round_weights(2)
            add_residual(0, x1_sb, (6, 7), x2_sb, xm_ps, x2_ready)
            statistics(2, x2_sb, 0)
            add_residual(1, x1_sb, (2, 3), x2_sb, xm_ps, x2_ready)
            statistics(2, x2_sb, 1)
            normalise(2, x2_sb, z3_sb, 0, z3_ready, 5)
            z_scales(0)
            normalise(2, x2_sb, z3_sb, 1, z3_ready, 6)
            z_scales(1)
            round_z(0)
            round_z(1)
            dve.wait_ge(wsb_out, 4)

            def scale_gate_up(n):
                b = n % 2
                for k in range(2):
                    i = 2 * n + k
                    cols = slice(k * FH, (k + 1) * FH)
                    dve.wait_ge(ffn_ps, i + 1)
                    if n >= 2:
                        dve.wait_ge(silu_done, i - 3)
                        dve.wait_ge(t_ready, i - 3)
                    v.tensor_tensor(g1[:, b, cols], bank[FFN_BANKS[i % 3][0]][:, 0:FH],
                                    wsb_gu[:, 0, cols], ALU.mult).then_inc(g1_ready, 1)
                    v.tensor_tensor(u1[:, b, cols], bank[FFN_BANKS[i % 3][1]][:, 0:FH],
                                    wsb_gu[:, 1, cols], ALU.mult).then_inc(u1_ready, 1)

            def activations(n):
                b = n % 2
                for k in range(2):
                    i = 2 * n + k
                    cols = slice(k * FH, (k + 1) * FH)
                    dve.wait_ge(silu_done, i + 1)
                    dve.wait_ge(u1_ready, i + 1)
                    if n >= 2:
                        dve.wait_ge(qt_ready, n - 1)
                    v.tensor_tensor(t_sb[:, b, cols], sg[:, b, cols], u1[:, b, cols],
                                    ALU.mult).then_inc(t_ready, 1)
                dve.wait_ge(t_ready, 2 * n + 2)
                step(v.tensor_reduce(t_max[:, n:n + 1], t_sb[:, b, :], AX.X, ALU.max, apply_absolute_value=True))
                step(v.tensor_scalar(t_scale[:, n:n + 1], t_max[:, n:n + 1], 1.0 / FP8_MAX, None, ALU.mult))
                v.reciprocal(t_inv[:, n:n + 1], t_scale[:, n:n + 1]).then_inc(t_inv_ready, 1)
                v.tensor_tensor(o_scale[:, n:n + 1], t_scale[:, n:n + 1], z_scale[:, n:n + 1], ALU.mult)

            def round_t(n):
                b = n % 2
                dve.wait_ge(t_big_ready, n + 1)
                if n >= 2:
                    dve.wait_ge(qtT_ps, n - 1)
                round_fp8(qt[:, b, 0:FF], t_val[:, b, :], t_big[:, b, :], qt_ready)

            def scale_output(n):
                dve.wait_ge(down_ps, n + 1)
                if n >= 2:
                    dve.wait_ge(y_ready, n - 1)
                v.scalar_tensor_tensor(o1[:, n % 2, :], bank[DOWN_BANK][:, 0:HID], o_scale[:, n:n + 1],
                                       wsb_d[:, :], ALU.mult, ALU.mult).then_inc(o1_ready, 1)

            for n in range(NT + 3):
                if n < NT:
                    scale_gate_up(n)
                if 1 <= n <= NT:
                    round_t(n - 1)
                if n < NT:
                    activations(n)
                if n >= 3:
                    scale_output(n - 3)


_INS = ["x", "ctx_1024", "L0_attn_weight_qkv", "L0_attn_weight_proj", "L0_xattn_Wq", "L0_xattn_bq",
        "L0_xattn_Wk", "L0_xattn_bk", "L0_ffn_w_gate", "L0_ffn_w_up", "L0_ffn_w_down",
        "L0_ffn_down_reorder_index"]


def kernel(**inputs):
    import numpy as _np
    import concourse.bacc as _bacc
    from concourse import mybir as _mybir
    from concourse.bass_utils import run_bass_kernel_spmd as _run

    nc = _bacc.Bacc("TRN2", target_bir_lowering=False, num_devices=1)
    arrays, args = {}, []
    for name in _INS:
        a = _np.ascontiguousarray(inputs[name])
        arrays[f"in_{name}_dram"] = a
        args.append(nc.dram_tensor(f"in_{name}_dram", a.shape, _mybir.dt.from_np(a.dtype), kind="ExternalInput").ap())
    args.append(nc.dram_tensor("out_0_dram", inputs["x"].shape, _mybir.dt.float32, kind="ExternalOutput").ap())
    decoder_layer_kernel(nc, *args)
    r = _run(nc, [arrays], core_ids=[0])
    return r.results[0]["out_0_dram"]
```

```python
import concourse.bass as bass
from concourse import mybir
from contextlib import ExitStack


def decoder_layer_kernel(nc, x, ctx_feat, w_qkv, w_proj, w_q, b_q, w_k, b_k,
                         w_gate, w_up, w_down, down_index, out):
    F32, BF16, I32 = mybir.dt.float32, mybir.dt.bfloat16, mybir.dt.int32
    ALU, ACT, AX = mybir.AluOpType, mybir.ActivationFunctionType, mybir.AxisListType

    P = 128
    SEQ, BATCH, HID = x.shape
    HALVES = BATCH // P
    NT = SEQ * HALVES
    KC = HID // P
    HD, KVH, QPK = 16, 4, 4
    HEADS = KVH * QPK
    KVD = KVH * HD
    QKV = HID + 2 * KVD
    PAIRS = SEQ * (SEQ + 1) // 2
    CD = ctx_feat.shape[2]
    CTXT = ctx_feat.shape[1] // P
    FF = w_gate.shape[0]
    FT = -(-FF // P)
    FLAST = FF - (FT - 1) * P
    FPAD = FT * P
    FH = FF // 2
    EPS = 1e-5
    FP8_MAX = 448.0
    SCALE = HD ** -0.5
    SHIFT = 2.0 ** 20
    EXP_BITS, HALF_BIT = 0x7F800000, 0x00400000
    M_LEAST = 1.5 * 2.0 ** 14

    first_pair = [q * (q + 1) // 2 for q in range(SEQ)]

    es = ExitStack()
    with es:
        def sb(name, shape, dt=F32):
            return es.enter_context(nc.sbuf_tensor(name, shape, dt))

        def sem(name):
            return es.enter_context(nc.semaphore(name))

        x_sb = sb("x_sb", [P, NT, HID])
        x1_sb = sb("x1_sb", [P, NT, HID])
        x2_sb = x1_sb
        z1_sb = sb("z1_sb", [P, NT, HID])
        z2_sb = sb("z2_sb", [P, NT, HID])
        z3_sb = z1_sb
        z1T = sb("z1T", [P, KC, NT * P])
        z2T = z1T
        ctx_sb = sb("ctx_sb", [P, SEQ * CTXT, CD])
        ctxT = sb("ctxT", [P, SEQ * CTXT * P])
        wqkv_sb = sb("wqkv_sb", [P, QKV // P, HID])
        wqkvT = sb("wqkvT", [P, KC, QKV])
        wproj_sb = sb("wproj_sb", [P, KC, HID])
        wprojT = sb("wprojT", [P, KC, HID])
        wx_sb = sb("wx_sb", [P, 2, CD])
        wxT = sb("wxT", [P, 2, CD])
        bx_sb = sb("bx_sb", [P, 2])
        qkT = sb("qkT", [P, 2, SEQ * CTXT * P])
        kv_sb = sb("kv_sb", [P, NT, 2 * KVD])
        area = sb("area", [P, 3 * PAIRS * HID])
        prod = area[:, 0:PAIRS * HID].rearrange("p (k i) -> p k i", k=PAIRS)
        pv = area[:, PAIRS * HID:].rearrange("p (h k i) -> p h k i", h=HALVES, k=PAIRS)
        g1, sg, t_big = (area[:, i * 2 * FF:(i + 1) * 2 * FF].rearrange("p (b j) -> p b j", b=2)
                         for i in range(3))
        sc = sb("sc", [P, HALVES, SEQ, SEQ, HEADS])
        e_sb = sb("e_sb", [P, HALVES, SEQ, SEQ, HEADS])
        sc_max = sb("sc_max", [P, HALVES, SEQ, HEADS])
        sc_sum = sb("sc_sum", [P, HALVES, SEQ, HEADS])
        sc_inv = sb("sc_inv", [P, HALVES, SEQ, HEADS])
        attT = z1_sb[:, :, :].rearrange("p n i -> p (n i)").rearrange(
            "p (h c t) -> p h c t", h=HALVES, c=KC)
        stats = sb("stats", [P, 3, NT, 6])
        mv = sb("mv", [P, 3, NT, 2])
        veps = sb("veps", [P, 3, NT])
        rstd = sb("rstd", [P, 3, NT])
        neg_half = sb("neg_half", [P, SEQ])
        neg_mean = sb("neg_mean", [P, 3, NT])
        shift = sb("shift", [P, 3, NT])
        fp8_div = sb("fp8_div", [P, 2])
        negmax = sb("negmax", [P, SEQ * CTXT])
        xa_sum = sb("xa_sum", [P, SEQ * CTXT])
        xa_inv = sb("xa_inv", [P, SEQ * CTXT])
        xa_T = qkT[:, :, :].rearrange("p a n -> p (a n)").rearrange(
            "p (s c m) -> p s c m", s=SEQ, c=CTXT)
        xa_exp = sb("xa_exp", [P, SEQ * CTXT, SEQ * 64])
        xa_prob = xa_exp
        idx_sb = sb("idx_sb", [P, FT], I32)
        wgu_sb = sb("wgu_sb", [P, 2, FT, HID])
        wd_sb = sb("wd_sb", [P, KC, FF])
        w_max = sb("w_max", [P, 2 * FT + KC])
        w_scale = sb("w_scale", [P, 2 * FT + KC])
        w_inv = sb("w_inv", [P, 2 * FT + KC])
        w_big = sb("w_big", [P, 2, FT * HID])
        qgu = sb("qgu", [P, 2, FT * HID], BF16)
        qwd = sb("qwd", [P, KC, FPAD], BF16)
        qguT = sb("qguT", [P, KC, 2, FF], BF16)
        qwdT = sb("qwdT", [P, FT, HID], BF16)
        diag = sb("diag", [P, 2 * FT + KC, P])
        wsb_gu = sb("wsb_gu", [P, 2, FF])
        wsb_d = sb("wsb_d", [P, HID])
        z_max = sb("z_max", [P, NT])
        z_scale = sb("z_scale", [P, NT])
        z_inv = sb("z_inv", [P, NT])
        z_val = z3_sb
        z_big = z2_sb
        qx = sb("qx", [P, NT, HID], BF16)
        qxT = sb("qxT", [P, NT, KC, P], BF16)
        t_sb = sb("t_sb", [P, 2, FF])
        t_max = sb("t_max", [P, NT])
        t_scale = sb("t_scale", [P, NT, 2])
        t_inv = sb("t_inv", [P, NT, 2])
        o_scale = sb("o_scale", [P, NT])
        t_val = t_sb
        qt = sb("qt", [P, 2, FPAD], BF16)
        qtT = sb("qtT", [P, 2, FT, P], BF16)
        o1 = sb("o1", [P, 2, HID])
        wproj_ord = o1
        y_sb = x_sb
        ident = sb("ident", [P, P])
        identb = sb("identb", [P, P], BF16)
        ones = sb("ones", [P, P])

        bank = [es.enter_context(nc.psum_tensor(f"bank{i}", [P, 512], F32)) for i in range(8)]
        FFN_BANKS = [(0, 1), (2, 3)]
        QT_BANK, DOWN_BANK = 4, 5

        x_in = [sem(f"x_in{h}") for h in range(HALVES)]
        wqkv_in, wproj_in, wx_in, ctx_in, idx_in, wd_in, out_written = (
            sem(n) for n in ("wqkv_in", "wproj_in", "wx_in", "ctx_in", "idx_in", "wd_in",
                             "out_written"))
        wgu_in = [sem("gate_in"), sem("up_in")]
        wproj_ordered = sem("wproj_ordered")
        gp_step, consts_ready, tails_ready, rstd_ready, diag_ready, probs_x_ready, y_ready = (
            sem(n) for n in ("gp_step", "consts_ready", "tails_ready", "rstd_ready",
                             "diag_ready", "probs_x_ready", "y_ready"))
        sc_masked, sg_scaled, o_scale_ready = (sem(n) for n in ("sc_masked", "sg_scaled", "o_scale_ready"))
        z1_ready, z2_ready, z3_ready = (sem(n) for n in ("z1_ready", "z2_ready", "z3_ready"))
        (wT_ps, ctxT_ps, z1T_ps, qkT_ps, qkv_ps, energy_ps, wsb_ps, qwT_ps, attT_ps, proj_ps,
         z2T_ps, xm_ps, probsT_ps, qxT_ps, ffn_ps, qtT_ps, down_ps) = (
            sem(n) for n in ("wT_ps", "ctxT_ps", "z1T_ps", "qkT_ps", "qkv_ps", "energy_ps",
                             "wsb_ps", "qwT_ps", "attT_ps", "proj_ps", "z2T_ps", "xm_ps", "probsT_ps",
                             "qxT_ps", "ffn_ps", "qtT_ps", "down_ps"))
        (wT_out, ctxT_out, z1T_out, qkT_out, kv_out, xexp_done, exp_done, wsb_out, w_val_ready,
         w_big_ready, qwT_out, attT_out, z2T_out, z_val_ready, z_big_ready, qxT_out, silu_done,
         t_val_ready, t_big_ready, qtT_out, probsT_out) = (
            sem(n) for n in ("wT_out", "ctxT_out", "z1T_out", "qkT_out", "kv_out", "xexp_done",
                             "exp_done", "wsb_out", "w_val_ready", "w_big_ready", "qwT_out",
                             "attT_out", "z2T_out", "z_val_ready", "z_big_ready", "qxT_out",
                             "silu_done", "t_val_ready", "t_big_ready", "qtT_out", "probsT_out"))
        (dve_step, stats_ready, negmax_ready, q_used, centred, pv_ready, xa_inv_ready,
         w_scale_ready, w_round, x1_ready, x2_ready, z_inv_ready, qx_ready,
         g1_ready, t_ready, t_inv_ready, t_sum_ready, qt_ready, o1_ready) = (
            sem(n) for n in ("dve_step", "stats_ready", "negmax_ready", "q_used",
                             "centred", "pv_ready", "xa_inv_ready",
                             "w_scale_ready", "w_round", "x1_ready", "x2_ready", "z_inv_ready",
                             "qx_ready", "g1_ready", "t_ready", "t_inv_ready", "t_sum_ready",
                             "qt_ready", "o1_ready"))

        block = es.enter_context(nc.Block())

        @block.sync
        def _(sp):
            rows = w_qkv.rearrange("(g r d) i -> r g d i", g=KVH, r=QPK + 2)

            def load_x(h):
                sp.dma_start(x_sb[:, h * SEQ:(h + 1) * SEQ, :],
                             x[:, h * P:(h + 1) * P, :].rearrange("s p i -> p s i")).then_inc(x_in[h], 16)

            load_x(0)
            for r in range(QPK + 2):
                sp.dma_start(wqkv_sb[(r % 2) * KVD:(r % 2 + 1) * KVD, r // 2, :], rows[r]).then_inc(wqkv_in, 16)
            load_x(1)
            sp.dma_start(wproj_sb[:, :, :], w_proj.rearrange("(t p) i -> p t i", p=P)).then_inc(wproj_in, 16)
            sp.dma_start(wd_sb[:, :, :], w_down.rearrange("(t p) i -> p t i", p=P)).then_inc(wd_in, 16)
            for n in range(NT):
                h, s = n // SEQ, n % SEQ
                sp.wait_ge(y_ready, n + 1)
                sp.dma_start(out[s, h * P:(h + 1) * P, :], y_sb[:, n, :]).then_inc(out_written, 16)
            sp.wait_ge(out_written, 16 * NT)

        @block.gpsimd
        def _(gp):
            gp.memset(ident[:, :], 0.0).then_inc(gp_step, 1)
            gp.memset(identb[:, :], 0.0).then_inc(gp_step, 1)
            gp.memset(ones[:, :], 1.0).then_inc(consts_ready, 1)
            gp.memset(neg_half[:, :], -0.5).then_inc(consts_ready, 1)
            gp.memset(fp8_div[:, 0:1], 1.0 / FP8_MAX).then_inc(consts_ready, 1)
            gp.memset(fp8_div[:, 1:2], 1.0 / (FP8_MAX * SHIFT)).then_inc(consts_ready, 1)
            gp.wait_ge(gp_step, 2)
            gp.affine_select(out=ident[:, :], in_=ident[:, :], compare_op=ALU.not_equal, fill=1.0,
                             base=0, pattern=[[-1, P]], channel_multiplier=1).then_inc(consts_ready, 1)
            gp.affine_select(out=identb[:, :], in_=identb[:, :], compare_op=ALU.not_equal, fill=1.0,
                             base=0, pattern=[[-1, P]], channel_multiplier=1).then_inc(consts_ready, 1)
            gp.memset(sc[:, :, :, :, :], -3.0e38).then_inc(sc_masked, 1)
            gp.memset(wgu_sb[:, :, FT - 1, :], 1.0).then_inc(tails_ready, 1)
            gp.wait_ge(consts_ready, 6)

            halves = [0]

            def inverse_deviation(ln, h):
                halves[0] += 1
                k = halves[0]
                sl = slice(h * SEQ, (h + 1) * SEQ)
                gp.wait_ge(stats_ready, k)
                gp.tensor_scalar(veps[:, ln, sl], mv[:, ln, sl, 1], EPS, 1.0, ALU.add, ALU.mult).then_inc(gp_step, 1)
                gp.tensor_scalar(neg_mean[:, ln, sl], mv[:, ln, sl, 0], -1.0, 1.0, ALU.mult, ALU.mult).then_inc(gp_step, 1)
                gp.wait_ge(gp_step, 3 * k)
                gp.tensor_tensor(rstd[:, ln, sl], veps[:, ln, sl], neg_half[:, :], ALU.pow).then_inc(gp_step, 1)
                gp.wait_ge(gp_step, 3 * k + 2)
                gp.tensor_tensor(shift[:, ln, sl], neg_mean[:, ln, sl], rstd[:, ln, sl], ALU.mult).then_inc(rstd_ready, 1)

            inverse_deviation(0, 0)
            inverse_deviation(0, 1)
            gp.wait_ge(idx_in, 32)
            gp.wait_ge(tails_ready, 1)
            for a, w in enumerate((w_gate, w_up)):
                for t in range(FT):
                    n = P if t < FT - 1 else FLAST
                    gp.indirect_dma_start(
                        wgu_sb[0:n, a, t, :], None, w,
                        bass.IndirectOffsetOnAxis(ap=idx_sb[0:n, t:t + 1], axis=0),
                    ).then_inc(wgu_in[a], 16)
            gp.wait_ge(wproj_in, 16)
            for t in range(KC):
                gp.tensor_copy(wproj_ord[:, t, :].rearrange("p (h g d) -> p h g d", g=KVH, h=QPK),
                               wproj_sb[:, t, :].rearrange("p (g h d) -> p h g d", g=KVH, h=QPK)
                               ).then_inc(wproj_ordered, 1)
            gp.memset(qwd[:, :, FF:FPAD], 0.0).then_inc(tails_ready, 1)
            gp.memset(qt[:, :, FF:FPAD], 0.0).then_inc(tails_ready, 1)
            for s in range(SEQ):
                gp.wait_ge(xa_inv_ready, s + 1)
                for t in range(CTXT):
                    i = s * CTXT + t
                    gp.tensor_scalar(xa_prob[:, i, :], xa_exp[:, i, :], xa_inv[:, i:i + 1], 1.0,
                                     ALU.mult, ALU.mult).then_inc(probs_x_ready, 1)
            gp.wait_ge(w_scale_ready, 1)
            for i in range(2 * FT + KC):
                gp.tensor_scalar(diag[:, i, :], ident[:, :], w_scale[:, i:i + 1], 1.0,
                                 ALU.mult, ALU.mult).then_inc(diag_ready, 1)
            inverse_deviation(1, 0)
            inverse_deviation(2, 0)
            inverse_deviation(1, 1)

            def scale_silu(n):
                for k in range(2):
                    cols = slice(k * FH, (k + 1) * FH)
                    gp.wait_ge(silu_done, 2 * n + k + 1)
                    gp.tensor_tensor(sg[:, n % 2, cols], sg[:, n % 2, cols], wsb_gu[:, 1, cols],
                                     ALU.mult).then_inc(sg_scaled, 1)

            def output_scale(n):
                gp.wait_ge(t_inv_ready, n + 1)
                gp.tensor_scalar(o_scale[:, n:n + 1], t_scale[:, n, 0:1], z_scale[:, n:n + 1], 1.0,
                                 ALU.mult, ALU.mult).then_inc(o_scale_ready, 1)

            def add_output(n):
                gp.wait_ge(o1_ready, n + 1)
                gp.tensor_tensor(y_sb[:, n, :], o1[:, n % 2, :], x2_sb[:, n, :], ALU.add).then_inc(y_ready, 1)

            gp.wait_ge(wsb_out, 4)
            for n in range(NT + 2):
                if n < NT:
                    scale_silu(n)
                    output_scale(n)
                if n == 0:
                    inverse_deviation(2, 1)
                if n >= 2:
                    add_output(n - 2)

        @block.tensor
        def _(pe):
            def norm_T(h, banks, src, done, normed, u):
                pe.wait_ge(normed, h * SEQ + 2 * u + 2)
                for c in range(KC):
                    for j in range(2):
                        last = pe.transpose(bank[banks[u]][:, (2 * c + j) * P:(2 * c + j + 1) * P],
                                            src[:, h * SEQ + 2 * u + j, c * P:(c + 1) * P], ident[:, :])
                last.then_inc(done, 1)

            def qkv(h, s):
                n = h * SEQ + s
                pe.wait_ge(z1T_out, 2 * h + s // 2 + 1)
                for c in range(KC):
                    last = pe.matmul(bank[4 * h + s][:, 0:QKV], z1T[:, c, n * P:(n + 1) * P], wqkvT[:, c, :],
                                     start=(c == 0), stop=(c == KC - 1))
                last.then_inc(qkv_ps, 1)

            def attention_T(h, banks, u):
                for c in range(KC):
                    for j in range(2):
                        q = 2 * u + j
                        if c == 0:
                            pe.wait_ge(pv_ready, h * SEQ + q + 1)
                        for k in range(q + 1):
                            last = pe.matmul(bank[banks[u]][:, (2 * c + j) * P:(2 * c + j + 1) * P],
                                             pv[:, h, first_pair[q] + k, c * P:(c + 1) * P],
                                             ident[:, :], start=(k == 0), stop=(k == q))
                last.then_inc(attT_ps, 1)

            def project(h, banks, u):
                pe.wait_ge(attT_out, 2 * h + u + 1)
                for j in range(2):
                    for c in range(KC):
                        last = pe.matmul(bank[banks[u]][:, j * HID:(j + 1) * HID],
                                         attT[:, h, c, (2 * u + j) * P:(2 * u + j + 1) * P], wprojT[:, c, :],
                                         start=(c == 0), stop=(c == KC - 1))
                last.then_inc(proj_ps, 1)

            def mix(h, banks, u):
                pe.wait_ge(z2T_out, 2 * h + u + 1)
                for j in range(2):
                    s = 2 * u + j
                    n = h * SEQ + s
                    for c in range(KC):
                        last = pe.matmul(bank[banks[u]][:, j * HID:(j + 1) * HID],
                                         z2T[:, c, n * P:(n + 1) * P], xa_T[:, s, c, :],
                                         start=(c == 0), stop=(c == KC - 1))
                last.then_inc(xm_ps, 1)

            def scales_row(u):
                if u < 2:
                    for t in range(4):
                        last = pe.matmul(bank[u][:, t * P:(t + 1) * P], ones[:, :], diag[:, u * FT + t, :],
                                         start=True, stop=True)
                elif u == 2:
                    for a in range(2):
                        at = a * (FF - 512)
                        pe.matmul(bank[0][:, at:at + P], ones[:, :], diag[:, a * FT + 4, :], start=True, stop=True)
                        last = pe.matmul(bank[0][:, at + P:at + P + FLAST], ones[0:FLAST, :],
                                         diag[0:FLAST, a * FT + 5, 0:FLAST], start=True, stop=True)
                else:
                    for t in range(KC):
                        last = pe.matmul(bank[1][:, t * P:(t + 1) * P], ones[:, :], diag[:, 2 * FT + t, :],
                                         start=True, stop=True)
                last.then_inc(wsb_ps, 1)

            def weights_T(a):
                pe.wait_ge(w_round, a + 1)
                for c in range(KC):
                    b = bank[2 + c][:, :].bitcast(BF16)
                    for t in range(FT):
                        rows = P if t < FT - 1 else FLAST
                        last = pe.transpose(b[:, t * P:t * P + rows],
                                            qgu[0:rows, a, t * HID + c * P:t * HID + (c + 1) * P],
                                            identb[0:rows, 0:rows])
                    last.then_inc(qwT_ps, 1)

            def down_weights_T():
                pe.wait_ge(w_round, 3)
                for u in range(2):
                    b = bank[2 + u][:, :].bitcast(BF16)
                    for j in range(3):
                        for t in range(KC):
                            last = pe.transpose(b[:, j * HID + t * P:j * HID + (t + 1) * P],
                                                qwd[:, t, (3 * u + j) * P:(3 * u + j + 1) * P], identb[:, :])
                    last.then_inc(qwT_ps, 1)

            def rounded_T(h, b):
                pe.wait_ge(qx_ready, h + 1)
                bb = bank[b][:, :].bitcast(BF16)
                for j in range(SEQ):
                    for c in range(KC):
                        k = j * KC + c
                        last = pe.transpose(bb[:, k * P:(k + 1) * P],
                                            qx[:, h * SEQ + j, c * P:(c + 1) * P], identb[:, :])
                last.then_inc(qxT_ps, 1)

            def gate_up(n, k):
                if n == 0:
                    pe.wait_ge(x2_ready, 2) if k == 0 else pe.wait_ge(qwT_out, 6)
                    pe.wait_ge(qxT_out, 1)
                    pe.wait_ge(qwT_out, 4)
                else:
                    pe.wait_ge(t_ready, 2 * (n - 1) + k + 1)
                    if n == SEQ:
                        pe.wait_ge(qxT_out, 2)
                for a in range(2):
                    for c in range(KC):
                        last = pe.matmul(bank[FFN_BANKS[k][a]][:, 0:FH], qxT[:, n, c, :],
                                         qguT[:, c, a, k * FH:(k + 1) * FH],
                                         start=(c == 0), stop=(c == KC - 1))
                last.then_inc(ffn_ps, 1)

            def activations_T(n):
                pe.wait_ge(qt_ready, n + 1)
                if n >= 1:
                    pe.wait_ge(qtT_out, n)
                bb = bank[QT_BANK][:, :].bitcast(BF16)
                for t in range(FT):
                    last = pe.transpose(bb[:, t * P:(t + 1) * P], qt[:, n % 2, t * P:(t + 1) * P], identb[:, :])
                last.then_inc(qtT_ps, 1)

            def down(n):
                pe.wait_ge(qtT_out, n + 1)
                if n >= 1:
                    pe.wait_ge(o1_ready, n)
                for t in range(FT):
                    last = pe.matmul(bank[DOWN_BANK][:, 0:HID], qtT[:, n % 2, t, :], qwdT[:, t, :],
                                     start=(t == 0), stop=(t == FT - 1))
                last.then_inc(down_ps, 1)

            pe.wait_ge(consts_ready, 6)
            pe.wait_ge(wqkv_in, 16 * (QPK + 2))
            for c in range(KC):
                for r in range(QKV // P):
                    last = pe.transpose(bank[4 + c][:, r * P:(r + 1) * P], wqkv_sb[:, r, c * P:(c + 1) * P], ident[:, :])
                last.then_inc(wT_ps, 1)
            norm_T(0, (6, 7), z1_sb, z1T_ps, z1_ready, 0)
            norm_T(0, (6, 7), z1_sb, z1T_ps, z1_ready, 1)
            pe.wait_ge(wT_out, 2)
            for s in range(SEQ):
                qkv(0, s)
            pe.wait_ge(wx_in, 64)
            for a in range(2):
                last = pe.transpose(bank[4][:, a * P:(a + 1) * P], wx_sb[:, a, :], ident[:, :])
            last.then_inc(wT_ps, 1)
            pe.wait_ge(ctx_in, 16)
            pe.wait_ge(z1T_out, 2)
            for u in range(2):
                for j in range(4):
                    last = pe.transpose(bank[6 + u][:, j * P:(j + 1) * P], ctx_sb[:, 4 * u + j, :], ident[:, :])
                last.then_inc(ctxT_ps, 1)
            pe.wait_ge(wT_out, 3)
            pe.wait_ge(ctxT_out, 2)
            for u in range(2):
                for a in range(2):
                    pe.matmul(bank[4 + 2 * u + a][:, :], wxT[:, a, :], ctxT[:, u * 512:(u + 1) * 512],
                              start=True, stop=True).then_inc(qkT_ps, 1)
            for s in range(SEQ):
                pe.wait_ge(qkT_out, 2 if s < 2 else 4)
                for t in range(CTXT):
                    last = pe.matmul(bank[4 + s][:, t * 256:(t + 1) * 256],
                                     qkT[:, 0, (s * CTXT + t) * P:(s * CTXT + t + 1) * P],
                                     qkT[:, 1, s * 256:(s + 1) * 256], start=True, stop=True)
                last.then_inc(energy_ps, 1)
            for u in range(2):
                pe.wait_ge(q_used, SEQ)
                norm_T(1, (0, 1), z1_sb, z1T_ps, z1_ready, u)
            for s in range(SEQ):
                pe.wait_ge(xexp_done, 2 * s + 2)
                qkv(1, s)
            pe.wait_ge(wproj_ordered, KC)
            for c in range(KC):
                for t in range(KC):
                    last = pe.transpose(bank[2][:, c * HID + t * P:c * HID + (t + 1) * P],
                                        wproj_ord[:, t, c * P:(c + 1) * P], ident[:, :])
            last.then_inc(wT_ps, 1)
            pe.wait_ge(z1T_out, 4)
            attention_T(0, (0, 1), 0)
            attention_T(0, (0, 1), 1)
            pe.wait_ge(wT_out, 4)
            project(0, (2, 3), 0)
            project(0, (2, 3), 1)
            for s in range(SEQ):
                if s < 2:
                    pe.wait_ge(attT_out, 2)
                else:
                    pe.wait_ge(probsT_out, s - 1)
                pe.wait_ge(probs_x_ready, (s + 1) * CTXT)
                for c in range(CTXT):
                    for t in range(CTXT):
                        last = pe.transpose(bank[s % 2][:, (c * CTXT + t) * P:(c * CTXT + t + 1) * P],
                                            xa_prob[:, s * CTXT + t, c * P:(c + 1) * P], ident[:, :])
                last.then_inc(probsT_ps, 1)
            pe.wait_ge(diag_ready, 2 * FT + KC)
            for u in range(2):
                pe.wait_ge(probsT_out, 3 + u)
                scales_row(u)
            for u in range(2):
                pe.wait_ge(wsb_out, 1 + u)
                scales_row(2 + u)
            for u in range(2):
                pe.wait_ge(x1_ready, u + 1)
                norm_T(0, (2, 3), z2_sb, z2T_ps, z2_ready, u)
            pe.wait_ge(wsb_out, 4)
            mix(0, (0, 1), 0)
            mix(0, (0, 1), 1)
            pe.wait_ge(q_used, 2 * SEQ)
            pe.wait_ge(kv_out, 2 * SEQ)
            attention_T(1, (4, 5), 0)
            attention_T(1, (4, 5), 1)
            project(1, (6, 7), 0)
            project(1, (6, 7), 1)
            pe.wait_ge(z2T_out, 2)
            weights_T(0)
            pe.wait_ge(qwT_out, 2)
            weights_T(1)
            pe.wait_ge(qwT_out, 4)
            down_weights_T()
            for u in range(2):
                pe.wait_ge(x1_ready, 3 + u)
                norm_T(1, (6, 7), z2_sb, z2T_ps, z2_ready, u)
            pe.wait_ge(attT_out, 3)
            rounded_T(0, QT_BANK)
            gate_up(0, 0)
            gate_up(0, 1)
            mix(1, (6, 7), 0)
            pe.wait_ge(z2T_out, 4)
            mix(1, (6, 7), 1)
            gate_up(1, 0)
            gate_up(1, 1)
            for n in range(1, NT + 1):
                if n == 1:
                    pe.wait_ge(qxT_out, 1)
                if n == 2:
                    pe.wait_ge(attT_out, 4)
                activations_T(n - 1)
                if n + 1 < NT:
                    if n + 1 == SEQ:
                        pe.wait_ge(x2_ready, 3)
                        rounded_T(1, 6)
                    gate_up(n + 1, 0)
                    down(n - 1)
                    gate_up(n + 1, 1)
                else:
                    down(n - 1)

        @block.scalar
        def _(act):
            if down_index.dtype == mybir.dt.int64:
                low = down_index.bitcast(I32).rearrange("(j w) -> j w", w=2)[:, 0:1]
            else:
                low = down_index.rearrange("(j w) -> j w", w=1)
            act.dma_start(idx_sb[:, 0:FT - 1],
                          low[0:(FT - 1) * P].rearrange("(t p) w -> p (t w)", p=P),
                          allow_slow_non_contiguous=True).then_inc(idx_in, 16)
            act.dma_start(idx_sb[0:FLAST, FT - 1:FT], low[(FT - 1) * P:FF]).then_inc(idx_in, 16)
            act.dma_start(wx_sb[:, 0, :], w_q).then_inc(wx_in, 16)
            act.dma_start(wx_sb[:, 1, :], w_k).then_inc(wx_in, 16)
            act.dma_start(bx_sb[:, 0:1], b_q.rearrange("(p w) -> p w", w=1)).then_inc(wx_in, 16)
            act.dma_start(bx_sb[:, 1:2], b_k.rearrange("(p w) -> p w", w=1)).then_inc(wx_in, 16)
            act.dma_start(ctx_sb[:, :, :], ctx_feat.rearrange("s (t p) c -> p (s t) c", p=P)).then_inc(ctx_in, 16)

            def copy(dst, src, scale=1.0):
                return act.activation(dst, src, ACT.Copy, scale=scale)

            halves = [0]

            def normalise(ln, src, dst, h, ready):
                halves[0] += 1
                act.wait_ge(rstd_ready, halves[0])
                for n in range(h * SEQ, (h + 1) * SEQ):
                    act.activation(dst[:, n, :], src[:, n, :], ACT.Identity, bias=shift[:, ln, n:n + 1],
                                   scale=rstd[:, ln, n:n + 1]).then_inc(ready, 1)

            def half_T(dst, h, banks, full, done):
                for u in range(2):
                    act.wait_ge(full, 2 * h + u + 1)
                    n = h * SEQ + 2 * u
                    copy(dst[:, :, n * P:(n + 2) * P],
                         bank[banks[u]][:, :].rearrange("p (c t) -> p c t", c=KC)).then_inc(done, 1)

            def attention_out(h, banks):
                for u in range(2):
                    act.wait_ge(attT_ps, 2 * h + u + 1)
                    copy(attT[:, h, :, 2 * u * P:2 * (u + 1) * P],
                         bank[banks[u]][:, :].rearrange("p (c t) -> p c t", c=KC)).then_inc(attT_out, 1)

            def keys_values(h):
                for s in range(SEQ):
                    act.wait_ge(qkv_ps, h * SEQ + s + 1)
                    copy(kv_sb[:, h * SEQ + s, :], bank[4 * h + s][:, HID:QKV]).then_inc(kv_out, 1)

            def exp_scores(h):
                act.wait_ge(centred, h + 1)
                act.activation(e_sb[:, h], sc[:, h], ACT.Exp, scale=SCALE).then_inc(exp_done, 1)

            def over_scale(a):
                act.wait_ge(w_scale_ready, 1)
                tiles, width = (FT, HID) if a < 2 else (KC, FF)
                for t in range(tiles):
                    src = wgu_sb[:, a, t, :] if a < 2 else wd_sb[:, t, :]
                    i = a * FT + t
                    copy(src, src, scale=w_inv[:, i:i + 1]).then_inc(w_val_ready, 1)
                act.wait_ge(w_val_ready, (FT, 2 * FT, 2 * FT + KC)[a])
                src = wgu_sb[:, a] if a < 2 else wd_sb[:, :, :]
                if a == 2:
                    act.wait_ge(w_round, 1)
                copy(w_big[:, a % 2, 0:tiles * width].rearrange("p (t i) -> p t i", t=tiles), src,
                     scale=SHIFT).then_inc(w_big_ready, 1)

            def gate_up_weights(a):
                for c in range(KC):
                    act.wait_ge(qwT_ps, 2 * a + c + 1)
                    copy(qguT[:, c, a, :], bank[2 + c][:, :].bitcast(BF16)[:, 0:FF]).then_inc(qwT_out, 1)

            def z_over_scale(h):
                act.wait_ge(z_inv_ready, h + 1)
                for s in range(SEQ):
                    n = h * SEQ + s
                    copy(z_val[:, n, :], z3_sb[:, n, :], scale=z_inv[:, n:n + 1]).then_inc(z_val_ready, 1)
                act.wait_ge(z_val_ready, (h + 1) * SEQ)
                copy(z_big[:, h * SEQ:(h + 1) * SEQ, :], z_val[:, h * SEQ:(h + 1) * SEQ, :],
                     scale=SHIFT).then_inc(z_big_ready, 1)

            def z_T(h, b):
                act.wait_ge(qxT_ps, h + 1)
                copy(qxT[:, h * SEQ:(h + 1) * SEQ, :, :],
                     bank[b][:, :].bitcast(BF16).rearrange("p (n c t) -> p n c t", n=SEQ, c=KC)
                     ).then_inc(qxT_out, 1)

            def silu(n):
                for k in range(2):
                    act.wait_ge(g1_ready, 2 * n + k + 1)
                    if n >= 2:
                        act.wait_ge(t_ready, 2 * (n - 2) + k + 1)
                    act.activation(sg[:, n % 2, k * FH:(k + 1) * FH], g1[:, n % 2, k * FH:(k + 1) * FH],
                                   ACT.Silu, scale=z_scale[:, n:n + 1]).then_inc(silu_done, 1)

            def t_over_scale(n):
                act.wait_ge(t_inv_ready, n + 1)
                if n >= 2:
                    act.wait_ge(qt_ready, n - 1)
                copy(t_big[:, n % 2, :], t_sb[:, n % 2, :], scale=t_inv[:, n, 1:2]).then_inc(t_big_ready, 1)
                copy(t_val[:, n % 2, :], t_sb[:, n % 2, :], scale=t_inv[:, n, 0:1]).then_inc(t_val_ready, 1)

            def t_T(n):
                act.wait_ge(qtT_ps, n + 1)
                if n >= 2:
                    act.wait_ge(down_ps, n - 1)
                copy(qtT[:, n % 2, :, :],
                     bank[QT_BANK][:, :].bitcast(BF16)[:, 0:FPAD].rearrange("p (k t) -> p k t", k=FT)
                     ).then_inc(qtT_out, 1)

            for c in range(KC):
                act.wait_ge(wT_ps, c + 1)
                copy(wqkvT[:, c, :], bank[4 + c][:, 0:QKV]).then_inc(wT_out, 1)
            normalise(0, x_sb, z1_sb, 0, z1_ready)
            half_T(z1T, 0, (6, 7), z1T_ps, z1T_out)
            normalise(0, x_sb, z1_sb, 1, z1_ready)
            keys_values(0)
            act.wait_ge(wT_ps, 3)
            copy(wxT[:, :, :], bank[4][:, 0:2 * P].rearrange("p (a c) -> p a c", a=2)).then_inc(wT_out, 1)
            for u in range(2):
                act.wait_ge(ctxT_ps, u + 1)
                copy(ctxT[:, u * 512:(u + 1) * 512], bank[6 + u][:, :]).then_inc(ctxT_out, 1)
            for u in range(2):
                for a in range(2):
                    act.wait_ge(qkT_ps, 2 * u + a + 1)
                    act.activation(qkT[:, a, u * 512:(u + 1) * 512], bank[4 + 2 * u + a][:, :],
                                   ACT.Identity, bias=bx_sb[:, a:a + 1], scale=1.0).then_inc(qkT_out, 1)
            exp_scores(0)
            for s in range(SEQ):
                act.wait_ge(negmax_ready, s + 1)
                for t in range(CTXT):
                    i = s * CTXT + t
                    act.activation(xa_exp[:, i, :], bank[4 + s][:, t * 256:(t + 1) * 256], ACT.Exp,
                                   bias=negmax[:, i:i + 1], accum_out=xa_sum[:, i:i + 1]).then_inc(xexp_done, 1)
            half_T(z1T, 1, (0, 1), z1T_ps, z1T_out)
            keys_values(1)
            act.wait_ge(wT_ps, 4)
            copy(wprojT[:, :, :], bank[2][:, :].rearrange("p (a c) -> p a c", a=KC)).then_inc(wT_out, 1)
            attention_out(0, (0, 1))
            for s in range(SEQ):
                act.wait_ge(probsT_ps, s + 1)
                copy(xa_T[:, s, :, :],
                     bank[s % 2][:, :].rearrange("p (c m) -> p c m", c=CTXT)).then_inc(probsT_out, 1)
            over_scale(0)
            exp_scores(1)
            for a in range(2):
                act.wait_ge(wsb_ps, a + 1)
                copy(wsb_gu[:, a, 0:512], bank[a][:, :]).then_inc(wsb_out, 1)
            act.wait_ge(wsb_ps, 3)
            copy(wsb_gu[:, :, 512:FF],
                 bank[0][:, 0:2 * (FF - 512)].rearrange("p (a c) -> p a c", a=2)).then_inc(wsb_out, 1)
            act.wait_ge(wsb_ps, 4)
            copy(wsb_d[:, :], bank[1][:, 0:HID]).then_inc(wsb_out, 1)
            normalise(1, x1_sb, z2_sb, 0, z2_ready)
            half_T(z2T, 0, (2, 3), z2T_ps, z2T_out)
            over_scale(1)
            attention_out(1, (4, 5))
            gate_up_weights(0)
            normalise(2, x2_sb, z3_sb, 0, z3_ready)
            gate_up_weights(1)
            over_scale(2)
            normalise(1, x1_sb, z2_sb, 1, z2_ready)
            z_over_scale(0)
            for u in range(2):
                act.wait_ge(qwT_ps, 5 + u)
                copy(qwdT[:, 3 * u:3 * u + 3, :],
                     bank[2 + u][:, :].bitcast(BF16)[:, 0:3 * HID].rearrange("p (t o) -> p t o", t=3)
                     ).then_inc(qwT_out, 1)
            half_T(z2T, 1, (6, 7), z2T_ps, z2T_out)
            z_T(0, QT_BANK)
            for n in range(NT + 1):
                if n < NT:
                    silu(n)
                if n == 1:
                    normalise(2, x2_sb, z3_sb, 1, z3_ready)
                if n >= 1:
                    t_T(n - 1)
                if n == 2:
                    z_over_scale(1)
                if n == 3:
                    z_T(1, 6)
                if n < NT:
                    t_over_scale(n)

        @block.vector
        def _(dve):
            v = nc.vector
            steps = [0]

            def step(ins):
                steps[0] += 1
                ins.then_inc(dve_step, 1)
                dve.wait_ge(dve_step, steps[0])

            def statistics(ln, src, h):
                for n in range(h * SEQ, (h + 1) * SEQ):
                    last = v.bn_stats(stats[:, ln, n, :], src[:, n, :])
                step(last)
                for n in range(h * SEQ, (h + 1) * SEQ):
                    last = v.bn_aggr(mv[:, ln, n, :], stats[:, ln, n, :])
                last.then_inc(stats_ready, 1)

            def query_key(h):
                dve.wait_ge(sc_masked, 1)
                for q in range(SEQ):
                    nk = q + 1
                    dve.wait_ge(kv_out, h * SEQ + q + 1)
                    pr = prod[:, first_pair[q]:first_pair[q] + nk, :]
                    v.tensor_tensor(
                        pr.rearrange("p k (h e) -> p k h e", h=QPK),
                        bank[4 * h + q][:, 0:HID].rearrange("p (h e) -> p h e", h=QPK).unsqueeze(1)
                        .broadcast_to([P, nk, QPK, KVD]),
                        kv_sb[:, h * SEQ:h * SEQ + nk, 0:KVD].unsqueeze(2).broadcast_to([P, nk, QPK, KVD]),
                        ALU.mult).then_inc(q_used, 1)
                for q in range(SEQ):
                    nk = q + 1
                    if q == 0:
                        dve.wait_ge(q_used, (h + 1) * SEQ)
                    pr = prod[:, first_pair[q]:first_pair[q] + nk, :]
                    last = v.tensor_reduce(sc[:, h, q, 0:nk, :], pr.rearrange("p k (c d) -> p k c d", d=HD),
                                           AX.X, ALU.add)
                step(last)
                step(v.tensor_reduce(sc_max[:, h], sc[:, h].rearrange("p q k c -> p q c k"), AX.X, ALU.max))
                v.tensor_tensor(sc[:, h], sc[:, h],
                                sc_max[:, h].unsqueeze(2).broadcast_to([P, SEQ, SEQ, HEADS]),
                                ALU.subtract).then_inc(centred, 1)

            def weighted_values(h):
                dve.wait_ge(exp_done, h + 1)
                step(v.tensor_reduce(sc_sum[:, h], e_sb[:, h].rearrange("p q k c -> p q c k"), AX.X, ALU.add))
                step(v.reciprocal(sc_inv[:, h], sc_sum[:, h]))
                step(v.tensor_tensor(e_sb[:, h], e_sb[:, h],
                                     sc_inv[:, h].unsqueeze(2).broadcast_to([P, SEQ, SEQ, HEADS]), ALU.mult))
                for q in range(SEQ):
                    nk = q + 1
                    full = [P, nk, QPK, KVH, HD]
                    v.tensor_tensor(
                        pv[:, h, first_pair[q]:first_pair[q] + nk, :].rearrange("p k (h g d) -> p k h g d", h=QPK, g=KVH),
                        e_sb[:, h, q, 0:nk, :].rearrange("p k (h g) -> p k h g", h=QPK).unsqueeze(4).broadcast_to(full),
                        kv_sb[:, h * SEQ:h * SEQ + nk, KVD:2 * KVD].rearrange("p k (g d) -> p k g d", g=KVH)
                        .unsqueeze(2).broadcast_to(full),
                        ALU.mult).then_inc(pv_ready, 1)

            def negate_maxima():
                for s in range(SEQ):
                    dve.wait_ge(energy_ps, s + 1)
                    v.tensor_reduce(negmax[:, s * CTXT:(s + 1) * CTXT],
                                    bank[4 + s][:, :].rearrange("p (t m) -> p t m", t=CTXT),
                                    AX.X, ALU.max, negate=True).then_inc(negmax_ready, 1)

            def context_sums():
                for s in range(SEQ):
                    dve.wait_ge(xexp_done, (s + 1) * CTXT)
                    v.reciprocal(xa_inv[:, s * CTXT:(s + 1) * CTXT],
                                 xa_sum[:, s * CTXT:(s + 1) * CTXT]).then_inc(xa_inv_ready, 1)

            def weight_scales():
                dve.wait_ge(wd_in, 16)
                v.tensor_reduce(w_max[:, 2 * FT:], wd_sb[:, :, :], AX.X, ALU.max, apply_absolute_value=True)
                for a in range(2):
                    dve.wait_ge(wgu_in[a], 16 * FT)
                    last = v.tensor_reduce(w_max[:, a * FT:(a + 1) * FT], wgu_sb[:, a], AX.X, ALU.max,
                                           apply_absolute_value=True)
                step(last)
                step(v.tensor_scalar(w_scale[:, :], w_max[:, :], 1.0 / FP8_MAX, None, ALU.mult))
                v.reciprocal(w_inv[:, :], w_scale[:, :]).then_inc(w_scale_ready, 1)

            def round_fp8(dst, val, big, ready):
                step(v.tensor_scalar(big.bitcast(I32), big.bitcast(I32), EXP_BITS, HALF_BIT,
                                     ALU.bitwise_and, ALU.bitwise_or))
                step(v.scalar_tensor_tensor(val, big, M_LEAST, val, ALU.max, ALU.add))
                v.scalar_tensor_tensor(dst, big, M_LEAST, val, ALU.max, ALU.subtract).then_inc(ready, 1)

            def round_weights(a):
                dve.wait_ge(w_big_ready, a + 1)
                if a < 2:
                    round_fp8(qgu[:, a, :], wgu_sb[:, a].rearrange("p t i -> p (t i)"), w_big[:, a, :], w_round)
                else:
                    round_fp8(qwd[:, :, 0:FF], wd_sb[:, :, :],
                              w_big[:, 0, 0:KC * FF].rearrange("p (t i) -> p t i", t=KC), w_round)

            def add_residual(h, base, banks, dst, full, ready):
                for u in range(2):
                    dve.wait_ge(full, 2 * h + u + 1)
                    n = h * SEQ + 2 * u
                    v.tensor_tensor(dst[:, n:n + 2, :],
                                    bank[banks[u]][:, :].rearrange("p (j i) -> p j i", j=2),
                                    base[:, n:n + 2, :], ALU.add).then_inc(ready, 1)
                dve.wait_ge(ready, 2 * h + 2)

            def z_scales(h):
                sl = slice(h * SEQ, (h + 1) * SEQ)
                dve.wait_ge(z3_ready, (h + 1) * SEQ)
                step(v.tensor_reduce(z_max[:, sl], z3_sb[:, sl, :], AX.X, ALU.max, apply_absolute_value=True))
                step(v.tensor_scalar(z_scale[:, sl], z_max[:, sl], 1.0 / FP8_MAX, None, ALU.mult))
                v.reciprocal(z_inv[:, sl], z_scale[:, sl]).then_inc(z_inv_ready, 1)

            def round_z(h):
                sl = slice(h * SEQ, (h + 1) * SEQ)
                dve.wait_ge(z_big_ready, h + 1)
                round_fp8(qx[:, sl, :], z_val[:, sl, :], z_big[:, sl, :], qx_ready)

            def scale_gate(n):
                for k in range(2):
                    i = 2 * n + k
                    cols = slice(k * FH, (k + 1) * FH)
                    dve.wait_ge(ffn_ps, i + 1)
                    if n >= 2:
                        dve.wait_ge(silu_done, i - 3)
                    v.tensor_tensor(g1[:, n % 2, cols], bank[FFN_BANKS[k][0]][:, 0:FH],
                                    wsb_gu[:, 0, cols], ALU.mult).then_inc(g1_ready, 1)

            def activations(n):
                b = n % 2
                if n >= 2:
                    dve.wait_ge(qt_ready, n - 1)
                for k in range(2):
                    i = 2 * n + k
                    cols = slice(k * FH, (k + 1) * FH)
                    dve.wait_ge(sg_scaled, i + 1)
                    v.tensor_tensor(t_sb[:, b, cols], bank[FFN_BANKS[k][1]][:, 0:FH], sg[:, b, cols],
                                    ALU.mult).then_inc(t_ready, 1)
                dve.wait_ge(t_ready, 2 * n + 2)
                step(v.tensor_reduce(t_max[:, n:n + 1], t_sb[:, b, :], AX.X, ALU.max, apply_absolute_value=True))
                step(v.tensor_scalar(t_scale[:, n, :], fp8_div[:, :], t_max[:, n:n + 1], None, ALU.mult))
                v.reciprocal(t_inv[:, n, :], t_scale[:, n, :]).then_inc(t_inv_ready, 1)

            def round_t(n):
                b = n % 2
                big = t_big[:, b, :]
                dve.wait_ge(t_big_ready, n + 1)
                step(v.tensor_scalar(big.bitcast(I32), big.bitcast(I32), EXP_BITS, HALF_BIT,
                                     ALU.bitwise_and, ALU.bitwise_or))
                dve.wait_ge(t_val_ready, n + 1)
                step(v.scalar_tensor_tensor(t_val[:, b, :], big, M_LEAST, t_val[:, b, :], ALU.max, ALU.add))
                if n >= 2:
                    dve.wait_ge(qtT_ps, n - 1)
                v.scalar_tensor_tensor(qt[:, b, 0:FF], big, M_LEAST, t_val[:, b, :],
                                       ALU.max, ALU.subtract).then_inc(qt_ready, 1)

            def scale_output(n):
                dve.wait_ge(down_ps, n + 1)
                dve.wait_ge(o_scale_ready, n + 1)
                if n >= 2:
                    dve.wait_ge(y_ready, n - 1)
                v.scalar_tensor_tensor(o1[:, n % 2, :], bank[DOWN_BANK][:, 0:HID], o_scale[:, n:n + 1],
                                       wsb_d[:, :], ALU.mult, ALU.mult).then_inc(o1_ready, 1)

            for h in range(HALVES):
                dve.wait_ge(x_in[h], 16)
                statistics(0, x_sb, h)
            query_key(0)
            negate_maxima()
            weighted_values(0)
            context_sums()
            weight_scales()
            query_key(1)
            add_residual(0, x_sb, (2, 3), x1_sb, proj_ps, x1_ready)
            statistics(1, x1_sb, 0)
            weighted_values(1)
            dve.wait_ge(tails_ready, 3)
            round_weights(0)
            add_residual(0, x1_sb, (0, 1), x2_sb, xm_ps, x2_ready)
            statistics(2, x2_sb, 0)
            round_weights(1)
            add_residual(1, x_sb, (6, 7), x1_sb, proj_ps, x1_ready)
            statistics(1, x1_sb, 1)
            z_scales(0)
            round_weights(2)
            round_z(0)
            dve.wait_ge(wsb_out, 4)
            dve.wait_ge(consts_ready, 6)
            for n in range(NT + 2):
                if n < NT:
                    scale_gate(n)
                if n == 1:
                    add_residual(1, x1_sb, (6, 7), x2_sb, xm_ps, x2_ready)
                    statistics(2, x2_sb, 1)
                if n >= 2:
                    scale_output(n - 2)
                if 1 <= n <= NT:
                    round_t(n - 1)
                if n < NT:
                    activations(n)
                if n == 1:
                    z_scales(1)
                if n == 2:
                    round_z(1)


_INS = ["x", "ctx_1024", "L0_attn_weight_qkv", "L0_attn_weight_proj", "L0_xattn_Wq", "L0_xattn_bq",
        "L0_xattn_Wk", "L0_xattn_bk", "L0_ffn_w_gate", "L0_ffn_w_up", "L0_ffn_w_down",
        "L0_ffn_down_reorder_index"]


def kernel(**inputs):
    import numpy as _np
    import concourse.bacc as _bacc
    from concourse import mybir as _mybir
    from concourse.bass_utils import run_bass_kernel_spmd as _run

    nc = _bacc.Bacc("TRN2", target_bir_lowering=False, num_devices=1)
    arrays, args = {}, []
    for name in _INS:
        a = _np.ascontiguousarray(inputs[name])
        arrays[f"in_{name}_dram"] = a
        args.append(nc.dram_tensor(f"in_{name}_dram", a.shape, _mybir.dt.from_np(a.dtype), kind="ExternalInput").ap())
    args.append(nc.dram_tensor("out_0_dram", inputs["x"].shape, _mybir.dt.float32, kind="ExternalOutput").ap())
    decoder_layer_kernel(nc, *args)
    r = _run(nc, [arrays], core_ids=[0])
    return r.results[0]["out_0_dram"]
```

```python
import concourse.bass as bass
from concourse import mybir
from contextlib import ExitStack


def decoder_layer_kernel(nc, x, ctx_feat, w_qkv, w_proj, w_q, b_q, w_k, b_k,
                         w_gate, w_up, w_down, down_index, out):
    F32, BF16, I32 = mybir.dt.float32, mybir.dt.bfloat16, mybir.dt.int32
    ALU, ACT, AX = mybir.AluOpType, mybir.ActivationFunctionType, mybir.AxisListType

    P = 128
    SEQ, BATCH, HID = x.shape
    HALVES = BATCH // P
    NT = SEQ * HALVES
    KC = HID // P
    HD, KVH, QPK = 16, 4, 4
    HEADS = KVH * QPK
    KVD = KVH * HD
    QKV = HID + 2 * KVD
    PAIRS = SEQ * (SEQ + 1) // 2
    CD = ctx_feat.shape[2]
    CTXT = ctx_feat.shape[1] // P
    FF = w_gate.shape[0]
    FT = -(-FF // P)
    FLAST = FF - (FT - 1) * P
    FPAD = FT * P
    FH = FF // 2
    EPS = 1e-5
    SHARED_FROM = 3
    WARM_UP_START, WARM_UP_FFN, WARM_UP_LAST = 8, 6, 3
    FP8_MAX = 448.0
    SCALE = HD ** -0.5
    SHIFT = 2.0 ** 20
    EXP_BITS, HALF_BIT = 0x7F800000, 0x00400000
    M_LEAST = 1.5 * 2.0 ** 14

    first_pair = [q * (q + 1) // 2 for q in range(SEQ)]

    es = ExitStack()
    with es:
        def sb(name, shape, dt=F32):
            return es.enter_context(nc.sbuf_tensor(name, shape, dt))

        def sem(name):
            return es.enter_context(nc.semaphore(name))

        x_sb = sb("x_sb", [P, NT, HID])
        x1_sb = sb("x1_sb", [P, NT, HID])
        x2_sb = x1_sb
        z1_sb = sb("z1_sb", [P, NT, HID])
        z2_sb = sb("z2_sb", [P, NT, HID])
        z3_sb = z1_sb
        z1T = sb("z1T", [P, KC, NT * P])
        z2T = z1T
        ctx_sb = sb("ctx_sb", [P, SEQ * CTXT, CD])
        ctxT = sb("ctxT", [P, SEQ * CTXT * P])
        wqkv_sb = sb("wqkv_sb", [P, QKV // P, HID])
        wqkvT = sb("wqkvT", [P, KC, QKV])
        wproj_sb = sb("wproj_sb", [P, KC, HID])
        wprojT = sb("wprojT", [P, KC, HID])
        wx_sb = sb("wx_sb", [P, 2, CD])
        wxT = sb("wxT", [P, 2, CD])
        bx_sb = sb("bx_sb", [P, 2])
        qkT = sb("qkT", [P, 2, SEQ * CTXT * P])
        kv_sb = sb("kv_sb", [P, NT, 2 * KVD])
        area = sb("area", [P, 3 * PAIRS * HID])
        prod = area[:, 0:PAIRS * HID].rearrange("p (k i) -> p k i", k=PAIRS)
        pv = area[:, PAIRS * HID:].rearrange("p (h k i) -> p h k i", h=HALVES, k=PAIRS)
        g1, sg, t_big, t_val = (area[:, i * 2 * FF:(i + 1) * 2 * FF].rearrange("p (b j) -> p b j", b=2)
                                for i in range(4))
        QS = SEQ - 1
        sc = sb("sc", [P, HALVES, QS, SEQ, HEADS])
        e_sb = sb("e_sb", [P, HALVES, QS, SEQ, HEADS])
        sc_max = sb("sc_max", [P, HALVES, QS, HEADS])
        sc_sum = sb("sc_sum", [P, HALVES, QS, HEADS])
        sc_inv = sb("sc_inv", [P, HALVES, QS, HEADS])
        attT = z1_sb[:, :, :].rearrange("p n i -> p (n i)").rearrange(
            "p (h c t) -> p h c t", h=HALVES, c=KC)
        stats = sb("stats", [P, 3, NT, 6])
        mv = sb("mv", [P, 3, NT, 2])
        veps = sb("veps", [P, 3, NT])
        rstd = sb("rstd", [P, 3, NT])
        neg_half = sb("neg_half", [P, SEQ])
        neg_mean = sb("neg_mean", [P, 3, NT])
        shift = sb("shift", [P, 3, NT])
        fp8_div = sb("fp8_div", [P, 2])
        negmax = sb("negmax", [P, SEQ * CTXT])
        xa_sum = sb("xa_sum", [P, SEQ * CTXT])
        xa_inv = sb("xa_inv", [P, SEQ * CTXT])
        xa_T = qkT[:, :, :].rearrange("p a n -> p (a n)").rearrange(
            "p (s c m) -> p s c m", s=SEQ, c=CTXT)
        xa_exp = sb("xa_exp", [P, SEQ * CTXT, SEQ * 64])
        xa_prob = xa_exp
        idx_sb = sb("idx_sb", [P, FT], I32)
        wgu_sb = sb("wgu_sb", [P, 2, FT, HID])
        wd_sb = sb("wd_sb", [P, KC, FF])
        w_max = sb("w_max", [P, 2 * FT + KC])
        w_scale = sb("w_scale", [P, 2 * FT + KC])
        w_inv = sb("w_inv", [P, 2 * FT + KC])
        w_inv_big = sb("w_inv_big", [P, 2 * FT + KC])
        w_big = sb("w_big", [P, 2, FT * HID])
        wd_big = w_big[:, 0, 0:KC * FF].rearrange("p (t i) -> p t i", t=KC)
        wd_val = w_big[:, 1, 0:KC * FF].rearrange("p (t i) -> p t i", t=KC)
        qgu = sb("qgu", [P, 2, FT * HID], BF16)
        qwd = sb("qwd", [P, KC, FPAD], BF16)
        qguT = sb("qguT", [P, KC, 2, FF], BF16)
        qwdT = sb("qwdT", [P, FT, HID], BF16)
        diag = sb("diag", [P, 2 * FT + KC, P])
        wsb_gu = sb("wsb_gu", [P, 2, FF])
        wsb_d = sb("wsb_d", [P, HID])
        z_max = sb("z_max", [P, NT])
        z_scale = sb("z_scale", [P, NT])
        z_inv = sb("z_inv", [P, NT])
        z_inv_big = sb("z_inv_big", [P, NT])
        z_val = z3_sb
        z_big = z2_sb
        qx = sb("qx", [P, NT, HID], BF16)
        qxT = sb("qxT", [P, NT, KC, P], BF16)
        t_sb = sb("t_sb", [P, 2, FF])
        t_max = sb("t_max", [P, NT])
        t_scale = sb("t_scale", [P, NT, 2])
        t_inv = sb("t_inv", [P, NT, 2])
        o_scale = sb("o_scale", [P, NT])
        qt = sb("qt", [P, 2, FPAD], BF16)
        qtT = sb("qtT", [P, 2, FT, P], BF16)
        o1 = sb("o1", [P, 2, HID])
        wproj_ord = o1
        y_sb = x_sb
        ident = sb("ident", [P, P])
        identb = sb("identb", [P, P], BF16)
        ones = sb("ones", [P, P])
        warm = sb("warm", [P, 1])

        bank = [es.enter_context(nc.psum_tensor(f"bank{i}", [P, 512], F32)) for i in range(8)]
        FFN_BANKS = [(0, 1), (2, 3)]
        QT_BANK, DOWN_BANK = 6, 7
        X1_BANKS = [(6, 7), (4, 5)]
        XM_BANKS = [(0, 1), (6, 7)]
        QX_BANKS = [(6, 7), (4, 5)]
        QKV_BANKS = [(0, 1, 2, 3), (2, 3, 4, 5)]

        x_in = [sem(n) for n in ("x_in_tiles01", "x_in_tiles23", "x_in_half1")]
        wqkv_in, wproj_in, wx_in, ctx_in, idx_in, out_written = (
            sem(n) for n in ("wqkv_in", "wproj_in", "wx_in", "ctx_in", "idx_in",
                             "out_written"))
        wgu_in = [sem("gate_in"), sem("up_in")]
        wd_in = [sem("wd_tile0_in"), sem("wd_tile1_in")]
        wproj_ordered = sem("wproj_ordered")
        gp_step, consts_ready, tails_ready, rstd_ready, diag_ready, probs_x_ready, y_ready = (
            sem(n) for n in ("gp_step", "consts_ready", "tails_ready", "rstd_ready",
                             "diag_ready", "probs_x_ready", "y_ready"))
        sc_masked, sg_scaled, o_scale_ready = (sem(n) for n in ("sc_masked", "sg_scaled", "o_scale_ready"))
        z1_ready, z2_ready, z3_ready = ([sem(f"z{i}_first3"), sem(f"z{i}_last")] for i in (1, 2, 3))
        z_part = sem("z_part")
        (wT_ps, ctxT_ps, z1T_ps, qkT_ps, qkv_ps, energy_ps, wsb_ps, qwT_ps, attT_ps, proj_ps,
         z2T_ps, xm_ps, probsT_ps, qxT_ps, gate_ps, up_ps, qtT_ps, down_ps) = (
            sem(n) for n in ("wT_ps", "ctxT_ps", "z1T_ps", "qkT_ps", "qkv_ps", "energy_ps",
                             "wsb_ps", "qwT_ps", "attT_ps", "proj_ps", "z2T_ps", "xm_ps", "probsT_ps",
                             "qxT_ps", "gate_ps", "up_ps", "qtT_ps", "down_ps"))
        (wT_out, ctxT_out, z1T_out, qkT_out, kv_out, xexp_done, exp_done, wsb_out, w_val_ready,
         w_big_ready, qwT_out, attT_out, z2T_out, z_val_ready, z_big_ready, qxT_out, silu_done,
         t_val_ready, t_big_ready, qtT_out, probsT_out, down_scaled, pv0_ready, x1_out, wd_scaled) = (
            sem(n) for n in ("wT_out", "ctxT_out", "z1T_out", "qkT_out", "kv_out", "xexp_done",
                             "exp_done", "wsb_out", "w_val_ready", "w_big_ready", "qwT_out",
                             "attT_out", "z2T_out", "z_val_ready", "z_big_ready", "qxT_out",
                             "silu_done", "t_val_ready", "t_big_ready", "qtT_out", "probsT_out",
                             "down_scaled", "pv0_ready", "x1_out",
                             "wd_scaled"))
        (dve_step, up_step, wd_over_scale, stats_ready, negmax_ready, q_used, centred, pv_ready, xa_inv_ready,
         w_scale_ready, w_round, x2_ready, z_inv_ready, qx_ready,
         t_ready, t_inv_ready, t_magic, t_sum, t_max_ready, t_scale_ready, qt_ready, o1_ready, y_last_ready) = (
            sem(n) for n in ("dve_step", "up_step", "wd_over_scale", "stats_ready", "negmax_ready", "q_used",
                             "centred", "pv_ready", "xa_inv_ready",
                             "w_scale_ready", "w_round", "x2_ready", "z_inv_ready",
                             "qx_ready", "t_ready", "t_inv_ready", "t_magic", "t_sum", "t_max_ready", "t_scale_ready",
                             "qt_ready", "o1_ready", "y_last_ready"))

        g1_ready = [sem("g1_chunk0_ready"), sem("g1_chunk1_ready")]
        gate_out = sem("gate_chunk1_out")

        block = es.enter_context(nc.Block())

        def x1_ps(n):
            return bank[X1_BANKS[n // SEQ][n % SEQ // 2]][:, n % 2 * HID:(n % 2 + 1) * HID]

        def load_x(engine, h, lo, hi, landed):
            engine.dma_start(x_sb[:, h * SEQ + lo:h * SEQ + hi, :],
                             x[lo:hi, h * P:(h + 1) * P, :].rearrange("s p i -> p s i")).then_inc(landed, 16)

        @block.sync
        def _(sp):
            load_x(sp, 0, 0, 2, x_in[0])
            load_x(sp, 0, 2, SEQ, x_in[1])
            sp.dma_start(wqkv_sb[:, :, :], w_qkv.rearrange("(t p) i -> p t i", p=P)).then_inc(wqkv_in, 16)
            for t in range(KC):
                sp.dma_start(wd_sb[:, t, :], w_down[t * P:(t + 1) * P, :]).then_inc(wd_in[t], 16)
            load_x(sp, 1, 0, SEQ, x_in[2])
            sp.dma_start(ctx_sb[:, :, :], ctx_feat.rearrange("s (t p) c -> p (s t) c", p=P)).then_inc(ctx_in, 16)
            sp.dma_start(wx_sb[:, 0, :], w_q).then_inc(wx_in, 16)
            sp.dma_start(wx_sb[:, 1, :], w_k).then_inc(wx_in, 16)
            sp.dma_start(bx_sb[:, 0:1], b_q.rearrange("(p w) -> p w", w=1)).then_inc(wx_in, 16)
            sp.dma_start(bx_sb[:, 1:2], b_k.rearrange("(p w) -> p w", w=1)).then_inc(wx_in, 16)
            sp.dma_start(wproj_sb[:, :, :], w_proj.rearrange("(t p) i -> p t i", p=P)).then_inc(wproj_in, 16)
            for n in range(NT):
                h, s = n // SEQ, n % SEQ
                if n < NT - 2:
                    sp.wait_ge(y_ready, n + 1)
                else:
                    sp.wait_ge(y_last_ready, n - (NT - 2) + 1)
                sp.dma_start(out[s, h * P:(h + 1) * P, :], y_sb[:, n, :]).then_inc(out_written, 16)
            sp.wait_ge(out_written, 16 * NT)

        @block.gpsimd
        def _(gp):
            gp.memset(ident[:, :], 0.0).then_inc(gp_step, 1)
            gp.memset(identb[:, :], 0.0).then_inc(gp_step, 1)
            gp.memset(ones[:, :], 1.0).then_inc(consts_ready, 1)
            gp.memset(neg_half[:, :], -0.5).then_inc(consts_ready, 1)
            gp.memset(fp8_div[:, 0:1], 1.0 / FP8_MAX).then_inc(consts_ready, 1)
            gp.memset(fp8_div[:, 1:2], 1.0 / (FP8_MAX * SHIFT)).then_inc(consts_ready, 1)
            gp.wait_ge(gp_step, 2)
            gp.affine_select(out=ident[:, :], in_=ident[:, :], compare_op=ALU.not_equal, fill=1.0,
                             base=0, pattern=[[-1, P]], channel_multiplier=1).then_inc(consts_ready, 1)
            gp.affine_select(out=identb[:, :], in_=identb[:, :], compare_op=ALU.not_equal, fill=1.0,
                             base=0, pattern=[[-1, P]], channel_multiplier=1).then_inc(consts_ready, 1)
            gp.memset(qwd[:, :, FF:FPAD], 0.0).then_inc(tails_ready, 1)
            gp.memset(sc[:, :, :, :, :], -3.0e38).then_inc(sc_masked, 1)
            gp.memset(wgu_sb[:, :, FT - 1, :], 1.0).then_inc(tails_ready, 1)
            gp.wait_ge(consts_ready, 6)

            halves = [0]

            def inverse_deviation(ln, h):
                halves[0] += 1
                k = halves[0]
                sl = slice(h * SEQ, (h + 1) * SEQ)
                gp.wait_ge(stats_ready, k)
                gp.tensor_scalar(veps[:, ln, sl], mv[:, ln, sl, 1], EPS, 1.0, ALU.add, ALU.mult).then_inc(gp_step, 1)
                gp.tensor_scalar(neg_mean[:, ln, sl], mv[:, ln, sl, 0], -1.0, 1.0, ALU.mult, ALU.mult).then_inc(gp_step, 1)
                gp.wait_ge(gp_step, 3 * k)
                gp.tensor_tensor(rstd[:, ln, sl], veps[:, ln, sl], neg_half[:, :], ALU.pow).then_inc(gp_step, 1)
                gp.wait_ge(gp_step, 3 * k + 2)
                gp.tensor_tensor(shift[:, ln, sl], neg_mean[:, ln, sl], rstd[:, ln, sl], ALU.mult).then_inc(rstd_ready, 1)

            def normalise(ln, src, dst, h, ready):
                inverse_deviation(ln, h)
                n = (h + 1) * SEQ - 1
                if ln == 1:
                    gp.wait_ge(x1_out, 2 * h + 2)
                gp.tensor_scalar(dst[:, n, :], src[:, n, :], rstd[:, ln, n:n + 1], 1.0,
                                 ALU.mult, ALU.mult).then_inc(z_part, 1)
                gp.wait_ge(z_part, halves[0])
                gp.wait_ge(rstd_ready, halves[0])
                gp.tensor_scalar(dst[:, n, :], dst[:, n, :], shift[:, ln, n:n + 1], 1.0,
                                 ALU.add, ALU.mult).then_inc(ready[1], 1)

            normalise(0, x_sb, z1_sb, 0, z1_ready)
            gp.wait_ge(idx_in, 32)
            gp.wait_ge(tails_ready, 2)
            for a, w in enumerate((w_gate, w_up)):
                for t in range(FT):
                    n = P if t < FT - 1 else FLAST
                    gp.indirect_dma_start(
                        wgu_sb[0:n, a, t, :], None, w,
                        bass.IndirectOffsetOnAxis(ap=idx_sb[0:n, t:t + 1], axis=0),
                    ).then_inc(wgu_in[a], 16)
                if a == 0:
                    normalise(0, x_sb, z1_sb, 1, z1_ready)
            gp.wait_ge(wproj_in, 16)
            for t in range(KC):
                gp.tensor_copy(wproj_ord[:, t, :].rearrange("p (h g d) -> p h g d", g=KVH, h=QPK),
                               wproj_sb[:, t, :].rearrange("p (g h d) -> p h g d", g=KVH, h=QPK)
                               ).then_inc(wproj_ordered, 1)
            gp.memset(qt[:, :, FF:FPAD], 0.0).then_inc(tails_ready, 1)
            for s in range(SEQ):
                gp.wait_ge(xa_inv_ready, s + 1)
                for t in range(CTXT):
                    i = s * CTXT + t
                    gp.tensor_scalar(xa_prob[:, i, :], xa_exp[:, i, :], xa_inv[:, i:i + 1], 1.0,
                                     ALU.mult, ALU.mult).then_inc(probs_x_ready, 1)
            gp.wait_ge(w_scale_ready, 2)
            for i in range(2 * FT + KC):
                gp.tensor_scalar(diag[:, i, :], ident[:, :], w_scale[:, i:i + 1], 1.0,
                                 ALU.mult, ALU.mult).then_inc(diag_ready, 1)

            def over_scale(a):
                for t in range(FT):
                    i = a * FT + t
                    gp.wait_ge(w_big_ready, i + 1)
                    gp.tensor_scalar(wgu_sb[:, a, t, :], wgu_sb[:, a, t, :], w_inv[:, i:i + 1], 1.0,
                                     ALU.mult, ALU.mult).then_inc(w_val_ready, 1)

            def z_over_scale(h):
                for n in range(h * SEQ, (h + 1) * SEQ):
                    gp.wait_ge(z_big_ready, n + 1)
                    gp.tensor_scalar(z_val[:, n, :], z3_sb[:, n, :], z_inv[:, n:n + 1], 1.0,
                                     ALU.mult, ALU.mult).then_inc(z_val_ready, 1)

            over_scale(0)
            over_scale(1)
            normalise(1, x1_sb, z2_sb, 0, z2_ready)
            normalise(2, x2_sb, z3_sb, 0, z3_ready)
            z_over_scale(0)
            normalise(1, x1_sb, z2_sb, 1, z2_ready)

            def scale_silu(n):
                for k in range(2):
                    cols = slice(k * FH, (k + 1) * FH)
                    gp.wait_ge(silu_done, 2 * n + k + 1)
                    gp.tensor_tensor(sg[:, n % 2, cols], sg[:, n % 2, cols], wsb_gu[:, 1, cols],
                                     ALU.mult).then_inc(sg_scaled, 1)

            def scale_gate(n):
                gp.wait_ge(gate_out, n - SHARED_FROM + 1)
                gp.tensor_tensor(g1[:, n % 2, FH:FF], g1[:, n % 2, FH:FF], wsb_gu[:, 0, FH:FF],
                                 ALU.mult).then_inc(g1_ready[1], 1)

            def output_scale(n):
                gp.wait_ge(t_inv_ready, n + 1)
                gp.tensor_scalar(o_scale[:, n:n + 1], t_scale[:, n, 0:1], z_scale[:, n:n + 1], 1.0,
                                 ALU.mult, ALU.mult).then_inc(o_scale_ready, 1)

            def add_output(n):
                gp.wait_ge(down_scaled, n + 1)
                gp.tensor_tensor(o1[:, n % 2, :], o1[:, n % 2, :], wsb_d[:, :], ALU.mult).then_inc(o1_ready, 1)
                gp.wait_ge(o1_ready, n + 1)
                gp.tensor_tensor(y_sb[:, n, :], o1[:, n % 2, :], x2_sb[:, n, :], ALU.add).then_inc(y_ready, 1)

            gp.wait_ge(wsb_out, 4)
            scale_silu(0)
            for n in range(NT + 1):
                if n == 1:
                    normalise(2, x2_sb, z3_sb, 1, z3_ready)
                if n == 2:
                    z_over_scale(1)
                if n + 1 < NT:
                    scale_silu(n + 1)
                if 2 <= n < NT:
                    add_output(n - 2)
                if n < NT:
                    output_scale(n)
                if SHARED_FROM <= n + 2 < NT:
                    scale_gate(n + 2)

        @block.tensor
        def _(pe):
            def norm_T(h, banks, src, done, u):
                normed = z1_ready if src is z1_sb else z2_ready
                pe.wait_ge(normed[0], 3 * h + 2 + u)
                if u == 1:
                    pe.wait_ge(normed[1], h + 1)
                for c in range(KC):
                    for j in range(2):
                        last = pe.transpose(bank[banks[u]][:, (2 * c + j) * P:(2 * c + j + 1) * P],
                                            src[:, h * SEQ + 2 * u + j, c * P:(c + 1) * P], ident[:, :])
                last.then_inc(done, 1)

            def qkv(h, s):
                n = h * SEQ + s
                pe.wait_ge(z1T_out, 2 * h + s // 2 + 1)
                lo = HID if s == 0 else 0
                for c in range(KC):
                    last = pe.matmul(bank[QKV_BANKS[h][s]][:, lo:QKV], z1T[:, c, n * P:(n + 1) * P], wqkvT[:, c, lo:],
                                     start=(c == 0), stop=(c == KC - 1))
                last.then_inc(qkv_ps, 1)

            def attention_T(h, banks, u):
                for c in range(KC):
                    for j in range(2):
                        q = 2 * u + j
                        if c == 0:
                            pe.wait_ge(pv0_ready, h + 1) if q == 0 else pe.wait_ge(pv_ready, h * QS + q)
                        for k in range(q + 1):
                            last = pe.matmul(bank[banks[u]][:, (2 * c + j) * P:(2 * c + j + 1) * P],
                                             pv[:, h, first_pair[q] + k, c * P:(c + 1) * P],
                                             ident[:, :], start=(k == 0), stop=(k == q))
                last.then_inc(attT_ps, 1)

            def project(h, u):
                for j in range(2):
                    n = h * SEQ + 2 * u + j
                    pe.matmul(x1_ps(n), ident[:, :], x_sb[:, n, :], start=True, stop=False)
                    if j == 0:
                        pe.wait_ge(attT_out, 2 * h + u + 1)
                    for c in range(KC):
                        last = pe.matmul(x1_ps(n), attT[:, h, c, (2 * u + j) * P:(2 * u + j + 1) * P],
                                         wprojT[:, c, :], start=False, stop=(c == KC - 1))
                last.then_inc(proj_ps, 1)

            def mix(h, u):
                pe.wait_ge(z2T_out, 2 * h + u + 1)
                for j in range(2):
                    s = 2 * u + j
                    n = h * SEQ + s
                    for c in range(KC):
                        last = pe.matmul(bank[XM_BANKS[h][u]][:, j * HID:(j + 1) * HID],
                                         z2T[:, c, n * P:(n + 1) * P], xa_T[:, s, c, :],
                                         start=(c == 0), stop=(c == KC - 1))
                last.then_inc(xm_ps, 1)

            def scales_row(u):
                if u < 2:
                    for t in range(4):
                        last = pe.matmul(bank[2 + u][:, t * P:(t + 1) * P], ones[:, :], diag[:, u * FT + t, :],
                                         start=True, stop=True)
                elif u == 2:
                    for a in range(2):
                        at = a * (FF - 512)
                        pe.matmul(bank[2][:, at:at + P], ones[:, :], diag[:, a * FT + 4, :], start=True, stop=True)
                        last = pe.matmul(bank[2][:, at + P:at + P + FLAST], ones[0:FLAST, :],
                                         diag[0:FLAST, a * FT + 5, 0:FLAST], start=True, stop=True)
                else:
                    for t in range(KC):
                        last = pe.matmul(bank[3][:, t * P:(t + 1) * P], ones[:, :], diag[:, 2 * FT + t, :],
                                         start=True, stop=True)
                last.then_inc(wsb_ps, 1)

            def weights_T(a):
                pe.wait_ge(w_round, a + 2)
                for c in range(KC):
                    b = bank[2 * (1 - a) + c][:, :].bitcast(BF16)
                    for t in range(FT):
                        rows = P if t < FT - 1 else FLAST
                        last = pe.transpose(b[:, t * P:t * P + rows],
                                            qgu[0:rows, a, t * HID + c * P:t * HID + (c + 1) * P],
                                            identb[0:rows, 0:rows])
                    last.then_inc(qwT_ps, 1)

            def down_weights_T():
                pe.wait_ge(w_round, 1)
                for u in range(2):
                    b = bank[u][:, :].bitcast(BF16)
                    for j in range(3):
                        for t in range(KC):
                            last = pe.transpose(b[:, j * HID + t * P:j * HID + (t + 1) * P],
                                                qwd[:, t, (3 * u + j) * P:(3 * u + j + 1) * P], identb[:, :])
                    last.then_inc(qwT_ps, 1)

            def rounded_T(h, part, b):
                pe.wait_ge(qx_ready, 2 * h + part + 1)
                bb = bank[b][:, :].bitcast(BF16)
                k = 0
                for j in ((0,), (1, 2, 3))[part]:
                    for c in range(KC):
                        last = pe.transpose(bb[:, k * P:(k + 1) * P],
                                            qx[:, h * SEQ + j, c * P:(c + 1) * P], identb[:, :])
                        k += 1
                last.then_inc(qxT_ps, 1)

            def gate_or_up(n, a, k):
                for c in range(KC):
                    last = pe.matmul(bank[FFN_BANKS[k][a]][:, 0:FH], qxT[:, n, c, :],
                                     qguT[:, c, a, k * FH:(k + 1) * FH],
                                     start=(c == 0), stop=(c == KC - 1))
                return last

            def gate(n):
                for k in range(2):
                    if n == 0:
                        pe.wait_ge(x2_ready, 2)
                        pe.wait_ge(qxT_out, 1)
                        pe.wait_ge(qwT_out, 6)
                    else:
                        if k == 1 and n > SHARED_FROM:
                            pe.wait_ge(gate_out, n - SHARED_FROM)
                        else:
                            pe.wait_ge(g1_ready[k], n)
                        if n == 1:
                            pe.wait_ge(qxT_out, 2)
                        if n == SEQ:
                            pe.wait_ge(qxT_out, 3)
                        if n == SEQ + 1:
                            pe.wait_ge(qxT_out, 4)
                    gate_or_up(n, 0, k).then_inc(gate_ps, 1)

            def up(n):
                for k in range(2):
                    if n >= 1:
                        pe.wait_ge(t_ready, 2 * (n - 1) + k + 1)
                    gate_or_up(n, 1, k).then_inc(up_ps, 1)

            def activations_T(n):
                if n >= 1:
                    pe.wait_ge(qtT_out, n)
                parts = ((0, FT, QT_BANK),) if n < NT - 1 else ((0, FT // 2, QT_BANK), (FT // 2, FT, 4))
                for k, (lo, hi, b) in enumerate(parts):
                    pe.wait_ge(qt_ready, n + k + 1)
                    bb = bank[b][:, :].bitcast(BF16)
                    for t in range(lo, hi):
                        last = pe.transpose(bb[:, t * P:(t + 1) * P], qt[:, n % 2, t * P:(t + 1) * P], identb[:, :])
                    last.then_inc(qtT_ps, 1)

            def down(n):
                pe.wait_ge(qtT_out, n + 1)
                b = DOWN_BANK if n < NT - 1 else 5
                if 1 <= n < NT - 1:
                    pe.wait_ge(down_scaled, n)
                for t in range(FT):
                    if n == NT - 1 and t == FT // 2:
                        pe.wait_ge(qtT_out, n + 2)
                    last = pe.matmul(bank[b][:, 0:HID], qtT[:, n % 2, t, :], qwdT[:, t, :],
                                     start=(t == 0), stop=(t == FT - 1))
                last.then_inc(down_ps, 1)

            def keep_busy(count, b):
                for _ in range(count):
                    pe.matmul(bank[b][:, 0:P], ones[:, :], ident[:, :], start=True, stop=True)

            pe.wait_ge(consts_ready, 6)
            keep_busy(WARM_UP_START, 0)
            pe.wait_ge(wqkv_in, 16)
            for c in range(KC):
                for r in range(QKV // P):
                    last = pe.transpose(bank[4 + c][:, r * P:(r + 1) * P], wqkv_sb[:, r, c * P:(c + 1) * P], ident[:, :])
                last.then_inc(wT_ps, 1)
            norm_T(0, (6, 7), z1_sb, z1T_ps, 0)
            norm_T(0, (6, 7), z1_sb, z1T_ps, 1)
            pe.wait_ge(wT_out, 2)
            for s in range(SEQ):
                qkv(0, s)
            pe.wait_ge(wx_in, 64)
            for a in range(2):
                last = pe.transpose(bank[4][:, a * P:(a + 1) * P], wx_sb[:, a, :], ident[:, :])
            last.then_inc(wT_ps, 1)
            pe.wait_ge(ctx_in, 16)
            pe.wait_ge(z1T_out, 2)
            for u in range(2):
                for j in range(4):
                    last = pe.transpose(bank[6 + u][:, j * P:(j + 1) * P], ctx_sb[:, 4 * u + j, :], ident[:, :])
                last.then_inc(ctxT_ps, 1)
            for u in range(2):
                if u == 1:
                    pe.wait_ge(q_used, 1)
                pe.wait_ge(kv_out, u + 1)
                pe.wait_ge(pv0_ready, 1)
                norm_T(1, (0, 1), z1_sb, z1T_ps, u)
            pe.wait_ge(wT_out, 3)
            pe.wait_ge(ctxT_out, 2)
            for u in range(2):
                for a in range(2):
                    pe.matmul(bank[4 + 2 * u + a][:, :], wxT[:, a, :], ctxT[:, u * 512:(u + 1) * 512],
                              start=True, stop=True).then_inc(qkT_ps, 1)
            for s in range(2):
                pe.wait_ge(q_used, s + 2)
                pe.wait_ge(kv_out, s + 3)
                qkv(1, s)
            for s in range(SEQ):
                pe.wait_ge(qkT_out, 2 if s < 2 else 4)
                for t in range(CTXT):
                    last = pe.matmul(bank[4 + s][:, t * 256:(t + 1) * 256],
                                     qkT[:, 0, (s * CTXT + t) * P:(s * CTXT + t + 1) * P],
                                     qkT[:, 1, s * 256:(s + 1) * 256], start=True, stop=True)
                last.then_inc(energy_ps, 1)
            for s in range(2, SEQ):
                pe.wait_ge(xexp_done, 2 * s - 2)
                qkv(1, s)
            pe.wait_ge(wproj_ordered, KC)
            pe.wait_ge(xexp_done, 8)
            for c in range(KC):
                for t in range(KC):
                    last = pe.transpose(bank[6][:, c * HID + t * P:c * HID + (t + 1) * P],
                                        wproj_ord[:, t, c * P:(c + 1) * P], ident[:, :])
            last.then_inc(wT_ps, 1)
            pe.wait_ge(z1T_out, 4)
            attention_T(0, (0, 1), 0)
            attention_T(0, (0, 1), 1)
            pe.wait_ge(wT_out, 4)
            project(0, 0)
            project(0, 1)
            for s in range(SEQ):
                if s < 2:
                    pe.wait_ge(attT_out, 2)
                else:
                    pe.wait_ge(probsT_out, s - 1)
                pe.wait_ge(probs_x_ready, (s + 1) * CTXT)
                for c in range(CTXT):
                    for t in range(CTXT):
                        last = pe.transpose(bank[s % 2][:, (c * CTXT + t) * P:(c * CTXT + t + 1) * P],
                                            xa_prob[:, s * CTXT + t, c * P:(c + 1) * P], ident[:, :])
                last.then_inc(probsT_ps, 1)
            pe.wait_ge(q_used, 2 * QS)
            pe.wait_ge(kv_out, 2 * SEQ)
            attention_T(1, (2, 3), 0)
            attention_T(1, (2, 3), 1)
            for u in range(2):
                pe.wait_ge(probsT_out, 3 + u)
                norm_T(0, (0, 1), z2_sb, z2T_ps, u)
            mix(0, 0)
            mix(0, 1)
            pe.wait_ge(diag_ready, 2 * FT + KC)
            pe.wait_ge(attT_out, 4)
            scales_row(0)
            scales_row(1)
            project(1, 0)
            for u in range(2):
                pe.wait_ge(wsb_out, 1 + u)
                scales_row(2 + u)
            pe.wait_ge(x2_ready, 2)
            down_weights_T()
            project(1, 1)
            pe.wait_ge(wsb_out, 4)
            weights_T(0)
            pe.wait_ge(qwT_out, 2)
            weights_T(1)
            pe.wait_ge(x2_ready, 2)
            pe.wait_ge(qwT_out, 4)
            keep_busy(WARM_UP_FFN, 2)
            rounded_T(0, 0, QX_BANKS[0][0])
            rounded_T(0, 1, QX_BANKS[0][1])
            gate(0)
            up(0)
            gate(1)
            for u in range(2):
                pe.wait_ge(qxT_out, u + 1)
                norm_T(1, (6, 7), z2_sb, z2T_ps, u)
            gate(2)
            mix(1, 0)
            mix(1, 1)
            up(1)
            pe.wait_ge(x2_ready, 4)
            for n in range(1, NT + 1):
                if n + 2 < NT and n + 2 != SEQ:
                    gate(n + 2)
                if n + 1 < NT:
                    up(n + 1)
                if n + 2 == SEQ:
                    pe.wait_ge(x2_ready, 4)
                    rounded_T(1, 0, QX_BANKS[1][0])
                    rounded_T(1, 1, QX_BANKS[1][1])
                    gate(n + 2)
                if n == NT - 1:
                    pe.wait_ge(g1_ready[0], NT)
                    keep_busy(WARM_UP_LAST, 0)
                activations_T(n - 1)
                if n == NT - 1:
                    keep_busy(WARM_UP_LAST, 0)
                down(n - 1)

        @block.scalar
        def _(act):
            if down_index.dtype == mybir.dt.int64:
                low = down_index.bitcast(I32).rearrange("(j w) -> j w", w=2)[:, 0:1]
            else:
                low = down_index.rearrange("(j w) -> j w", w=1)
            act.dma_start(idx_sb[:, 0:FT - 1],
                          low[0:(FT - 1) * P].rearrange("(t p) w -> p (t w)", p=P),
                          allow_slow_non_contiguous=True).then_inc(idx_in, 16)
            act.dma_start(idx_sb[0:FLAST, FT - 1:FT], low[(FT - 1) * P:FF]).then_inc(idx_in, 16)

            def copy(dst, src, scale=1.0):
                return act.activation(dst, src, ACT.Copy, scale=scale)

            def normalise(ln, src, dst, h, ready, count):
                act.wait_ge(rstd_ready, count)
                for n in range(h * SEQ, h * SEQ + 3):
                    act.activation(dst[:, n, :], src[:, n, :], ACT.Identity, bias=shift[:, ln, n:n + 1],
                                   scale=rstd[:, ln, n:n + 1]).then_inc(ready[0], 1)

            def x1_out_of_psum(h, stats_count):
                act.wait_ge(stats_ready, stats_count)
                for u in range(2):
                    n = h * SEQ + 2 * u
                    copy(x1_sb[:, n:n + 2, :].rearrange("p n i -> p (n i)"), bank[X1_BANKS[h][u]][:, :]
                         ).then_inc(x1_out, 1)
                act.wait_ge(x1_out, 2 * h + 2)

            def half_T(dst, h, banks, full, done):
                for u in range(2):
                    act.wait_ge(full, 2 * h + u + 1)
                    n = h * SEQ + 2 * u
                    copy(dst[:, :, n * P:(n + 2) * P],
                         bank[banks[u]][:, :].rearrange("p (c t) -> p c t", c=KC)).then_inc(done, 1)

            def attention_out(h, u, b):
                act.wait_ge(attT_ps, 2 * h + u + 1)
                copy(attT[:, h, :, 2 * u * P:2 * (u + 1) * P],
                     bank[b][:, :].rearrange("p (c t) -> p c t", c=KC)).then_inc(attT_out, 1)

            def keys_values(h, s):
                act.wait_ge(qkv_ps, h * SEQ + s + 1)
                copy(kv_sb[:, h * SEQ + s, :], bank[QKV_BANKS[h][s]][:, HID:QKV]).then_inc(kv_out, 1)
                if s == 0:
                    copy(pv[:, h, 0, :].rearrange("p (h e) -> p h e", h=QPK),
                         bank[QKV_BANKS[h][s]][:, HID + KVD:QKV].unsqueeze(1).broadcast_to([P, QPK, KVD])
                         ).then_inc(pv0_ready, 1)

            def exp_scores(h):
                act.wait_ge(centred, h + 1)
                act.activation(e_sb[:, h], sc[:, h], ACT.Exp, scale=SCALE).then_inc(exp_done, 1)

            def over_scale(a):
                act.wait_ge(w_scale_ready, 2)
                if a == 0:
                    act.wait_ge(w_round, 1)
                for t in range(FT):
                    i = a * FT + t
                    copy(w_big[:, a, t * HID:(t + 1) * HID], wgu_sb[:, a, t, :],
                         scale=w_inv_big[:, i:i + 1]).then_inc(w_big_ready, 1)

            def gate_up_weights(a):
                for c in range(KC):
                    act.wait_ge(qwT_ps, 2 * a + c + 3)
                    copy(qguT[:, c, a, :], bank[2 * (1 - a) + c][:, :].bitcast(BF16)[:, 0:FF]).then_inc(qwT_out, 1)

            def z_over_scale(h):
                act.wait_ge(z_inv_ready, h + 1)
                for n in range(h * SEQ, (h + 1) * SEQ):
                    copy(z_big[:, n, :], z3_sb[:, n, :], scale=z_inv_big[:, n:n + 1]).then_inc(z_big_ready, 1)

            def z_T(h, part, b):
                act.wait_ge(qxT_ps, 2 * h + part + 1)
                lo, hi = (h * SEQ, h * SEQ + 1) if part == 0 else (h * SEQ + 1, (h + 1) * SEQ)
                copy(qxT[:, lo:hi, :, :],
                     bank[b][:, :].bitcast(BF16)[:, 0:(hi - lo) * HID].rearrange("p (n c t) -> p n c t", n=hi - lo, c=KC)
                     ).then_inc(qxT_out, 1)

            def silu(n):
                for k in range(2):
                    act.wait_ge(g1_ready[k], n + 1)
                    if n >= 2:
                        act.wait_ge(t_ready, 2 * (n - 2) + k + 1)
                    act.activation(sg[:, n % 2, k * FH:(k + 1) * FH], g1[:, n % 2, k * FH:(k + 1) * FH],
                                   ACT.Silu, scale=z_scale[:, n:n + 1]).then_inc(silu_done, 1)

            def gate_chunk_out(n):
                act.wait_ge(gate_ps, 2 * n + 2)
                act.wait_ge(silu_done, 2 * (n - 2) + 2)
                copy(g1[:, n % 2, FH:FF], bank[FFN_BANKS[1][0]][:, 0:FH]).then_inc(gate_out, 1)

            def t_over_scale(n):
                act.wait_ge(t_inv_ready, n + 1)
                if n >= 2:
                    act.wait_ge(qt_ready, n - 1)
                copy(t_big[:, n % 2, :], t_sb[:, n % 2, :], scale=t_inv[:, n, 1:2]).then_inc(t_big_ready, 1)
                for k in range(2):
                    cols = slice(k * FH, (k + 1) * FH)
                    copy(t_val[:, n % 2, cols], t_sb[:, n % 2, cols], scale=t_inv[:, n, 0:1]).then_inc(t_val_ready, 1)

            def t_T(n):
                if n >= 2:
                    act.wait_ge(down_ps, n - 1)
                parts = ((0, FT, QT_BANK),) if n < NT - 1 else ((0, FT // 2, QT_BANK), (FT // 2, FT, 4))
                for k, (lo, hi, b) in enumerate(parts):
                    act.wait_ge(qtT_ps, n + k + 1)
                    copy(qtT[:, n % 2, lo:hi, :],
                         bank[b][:, :].bitcast(BF16)[:, lo * P:hi * P].rearrange("p (k t) -> p k t", k=hi - lo)
                         ).then_inc(qtT_out, 1)

            def scale_down(n):
                act.wait_ge(down_ps, n + 1)
                act.wait_ge(o_scale_ready, n + 1)
                if n >= 2:
                    act.wait_ge(y_ready, n - 1)
                copy(o1[:, n % 2, :], bank[DOWN_BANK][:, 0:HID], scale=o_scale[:, n:n + 1]).then_inc(down_scaled, 1)

            act.wait_ge(consts_ready, 6)
            act.activation(warm[:, :], ones[:, 0:1], ACT.Exp)
            for c in range(KC):
                act.wait_ge(wT_ps, c + 1)
                copy(wqkvT[:, c, :].rearrange("p (r g d) -> p r g d", g=KVH, r=QPK + 2),
                     bank[4 + c][:, 0:QKV].rearrange("p (g r d) -> p r g d", g=KVH, r=QPK + 2)
                     ).then_inc(wT_out, 1)
            normalise(0, x_sb, z1_sb, 0, z1_ready, 1)
            half_T(z1T, 0, (6, 7), z1T_ps, z1T_out)
            act.wait_ge(w_scale_ready, 1)
            for t in range(KC):
                i = 2 * FT + t
                copy(wd_big[:, t, :], wd_sb[:, t, :], scale=w_inv_big[:, i:i + 1]).then_inc(wd_scaled, 1)
            for s in range(SEQ):
                keys_values(0, s)
            normalise(0, x_sb, z1_sb, 1, z1_ready, 2)
            act.wait_ge(wT_ps, 3)
            copy(wxT[:, :, :], bank[4][:, 0:2 * P].rearrange("p (a c) -> p a c", a=2)).then_inc(wT_out, 1)
            for u in range(2):
                act.wait_ge(ctxT_ps, u + 1)
                copy(ctxT[:, u * 512:(u + 1) * 512], bank[6 + u][:, :]).then_inc(ctxT_out, 1)
            half_T(z1T, 1, (0, 1), z1T_ps, z1T_out)
            for u in range(2):
                if u == 1:
                    exp_scores(0)
                for a in range(2):
                    act.wait_ge(qkT_ps, 2 * u + a + 1)
                    act.activation(qkT[:, a, u * 512:(u + 1) * 512], bank[4 + 2 * u + a][:, :],
                                   ACT.Identity, bias=bx_sb[:, a:a + 1], scale=1.0).then_inc(qkT_out, 1)
            for s in range(2):
                keys_values(1, s)
            for s in range(SEQ):
                act.wait_ge(negmax_ready, s + 1)
                for t in range(CTXT):
                    i = s * CTXT + t
                    act.activation(xa_exp[:, i, :], bank[4 + s][:, t * 256:(t + 1) * 256], ACT.Exp,
                                   bias=negmax[:, i:i + 1], accum_out=xa_sum[:, i:i + 1]).then_inc(xexp_done, 1)
            for s in range(2, SEQ):
                keys_values(1, s)
            act.wait_ge(wT_ps, 4)
            copy(wprojT[:, :, :], bank[6][:, :].rearrange("p (a c) -> p a c", a=KC)).then_inc(wT_out, 1)
            attention_out(0, 0, 0)
            over_scale(0)
            attention_out(0, 1, 1)
            over_scale(1)
            exp_scores(1)
            for s in range(SEQ):
                act.wait_ge(probsT_ps, s + 1)
                copy(xa_T[:, s, :, :],
                     bank[s % 2][:, :].rearrange("p (c m) -> p c m", c=CTXT)).then_inc(probsT_out, 1)
            act.activation(warm[:, :], ones[:, 0:1], ACT.Silu)
            x1_out_of_psum(0, 3)
            attention_out(1, 0, 2)
            normalise(1, x1_sb, z2_sb, 0, z2_ready, 3)
            attention_out(1, 1, 3)
            half_T(z2T, 0, (0, 1), z2T_ps, z2T_out)
            for a in range(2):
                act.wait_ge(wsb_ps, a + 1)
                copy(wsb_gu[:, a, 0:512], bank[2 + a][:, :]).then_inc(wsb_out, 1)
            normalise(2, x2_sb, z3_sb, 0, z3_ready, 4)
            act.wait_ge(wsb_ps, 3)
            copy(wsb_gu[:, :, 512:FF],
                 bank[2][:, 0:2 * (FF - 512)].rearrange("p (a c) -> p a c", a=2)).then_inc(wsb_out, 1)
            act.wait_ge(wsb_ps, 4)
            copy(wsb_d[:, :], bank[3][:, 0:HID]).then_inc(wsb_out, 1)
            for u in range(2):
                act.wait_ge(qwT_ps, 1 + u)
                copy(qwdT[:, 3 * u:3 * u + 3, :],
                     bank[u][:, :].bitcast(BF16)[:, 0:3 * HID].rearrange("p (t o) -> p t o", t=3)
                     ).then_inc(qwT_out, 1)
            z_over_scale(0)
            gate_up_weights(0)
            gate_up_weights(1)
            x1_out_of_psum(1, 5)
            z_T(0, 0, QX_BANKS[0][0])
            z_T(0, 1, QX_BANKS[0][1])
            silu(0)
            half_T(z2T, 1, (6, 7), z2T_ps, z2T_out)
            silu(1)
            for n in range(NT + 1):
                if n == 1:
                    normalise(2, x2_sb, z3_sb, 1, z3_ready, 6)
                if n == 2:
                    z_over_scale(1)
                if 1 <= n and n + 1 < NT:
                    silu(n + 1)
                if n == NT - 1:
                    t_over_scale(n)
                if 2 <= n < NT:
                    scale_down(n - 2)
                if n == 2:
                    z_T(1, 0, QX_BANKS[1][0])
                    z_T(1, 1, QX_BANKS[1][1])
                if n < NT - 1:
                    t_over_scale(n)
                if SHARED_FROM <= n + 2 < NT:
                    gate_chunk_out(n + 2)
                if n >= 1:
                    t_T(n - 1)

        @block.vector
        def _(dve):
            v = nc.vector
            steps = [0]

            def step(ins):
                steps[0] += 1
                ins.then_inc(dve_step, 1)
                dve.wait_ge(dve_step, steps[0])

            def tile_statistics(ln, tiles):
                for n in tiles:
                    h, s = n // SEQ, n % SEQ
                    if s % 2 == 0:
                        if ln == 0:
                            dve.wait_ge(x_in[2 if h else s // 2], 16)
                        elif ln == 1:
                            dve.wait_ge(proj_ps, n // 2 + 1)
                        else:
                            dve.wait_ge(x2_ready, n // 2 + 1)
                    last = v.bn_stats(stats[:, ln, n, :], (x_sb[:, n, :], x1_ps(n), x2_sb[:, n, :])[ln])
                return last

            def mean_variance(ln, h):
                for n in range(h * SEQ, (h + 1) * SEQ):
                    last = v.bn_aggr(mv[:, ln, n, :], stats[:, ln, n, :])
                last.then_inc(stats_ready, 1)

            def statistics(ln, h):
                step(tile_statistics(ln, range(h * SEQ, (h + 1) * SEQ)))
                mean_variance(ln, h)

            def query_key(h):
                dve.wait_ge(sc_masked, 1)
                for q in range(1, SEQ):
                    nk = q + 1
                    dve.wait_ge(kv_out, h * SEQ + q + 1)
                    pr = prod[:, first_pair[q]:first_pair[q] + nk, :]
                    v.tensor_tensor(
                        pr.rearrange("p k (h e) -> p k h e", h=QPK),
                        bank[QKV_BANKS[h][q]][:, 0:HID].rearrange("p (h e) -> p h e", h=QPK).unsqueeze(1)
                        .broadcast_to([P, nk, QPK, KVD]),
                        kv_sb[:, h * SEQ:h * SEQ + nk, 0:KVD].unsqueeze(2).broadcast_to([P, nk, QPK, KVD]),
                        ALU.mult).then_inc(q_used, 1)
                for q in range(1, SEQ):
                    nk = q + 1
                    if q == 1:
                        dve.wait_ge(q_used, (h + 1) * QS)
                    pr = prod[:, first_pair[q]:first_pair[q] + nk, :]
                    last = v.tensor_reduce(sc[:, h, q - 1, 0:nk, :], pr.rearrange("p k (c d) -> p k c d", d=HD),
                                           AX.X, ALU.add)
                step(last)
                step(v.tensor_reduce(sc_max[:, h], sc[:, h].rearrange("p q k c -> p q c k"), AX.X, ALU.max))
                v.tensor_tensor(sc[:, h], sc[:, h],
                                sc_max[:, h].unsqueeze(2).broadcast_to([P, QS, SEQ, HEADS]),
                                ALU.subtract).then_inc(centred, 1)

            def probabilities(h):
                dve.wait_ge(exp_done, h + 1)
                step(v.tensor_reduce(sc_sum[:, h], e_sb[:, h].rearrange("p q k c -> p q c k"), AX.X, ALU.add))
                step(v.reciprocal(sc_inv[:, h], sc_sum[:, h]))
                step(v.tensor_tensor(e_sb[:, h], e_sb[:, h],
                                     sc_inv[:, h].unsqueeze(2).broadcast_to([P, QS, SEQ, HEADS]), ALU.mult))

            def weighted_values(h, queries):
                for q in queries:
                    nk = q + 1
                    full = [P, nk, QPK, KVH, HD]
                    v.tensor_tensor(
                        pv[:, h, first_pair[q]:first_pair[q] + nk, :].rearrange("p k (h g d) -> p k h g d", h=QPK, g=KVH),
                        e_sb[:, h, q - 1, 0:nk, :].rearrange("p k (h g) -> p k h g", h=QPK).unsqueeze(4).broadcast_to(full),
                        kv_sb[:, h * SEQ:h * SEQ + nk, KVD:2 * KVD].rearrange("p k (g d) -> p k g d", g=KVH)
                        .unsqueeze(2).broadcast_to(full),
                        ALU.mult).then_inc(pv_ready, 1)

            def negate_maxima(batches):
                for s in batches:
                    dve.wait_ge(energy_ps, s + 1)
                    v.tensor_reduce(negmax[:, s * CTXT:(s + 1) * CTXT],
                                    bank[4 + s][:, :].rearrange("p (t m) -> p t m", t=CTXT),
                                    AX.X, ALU.max, negate=True).then_inc(negmax_ready, 1)

            def context_sums():
                for s in range(SEQ):
                    dve.wait_ge(xexp_done, (s + 1) * CTXT)
                    v.reciprocal(xa_inv[:, s * CTXT:(s + 1) * CTXT],
                                 xa_sum[:, s * CTXT:(s + 1) * CTXT]).then_inc(xa_inv_ready, 1)

            def weight_scales(lo, hi):
                step(v.tensor_scalar(w_scale[:, lo:hi], w_max[:, lo:hi], 1.0 / FP8_MAX, None, ALU.mult))
                step(v.reciprocal(w_inv[:, lo:hi], w_scale[:, lo:hi]))
                v.tensor_scalar(w_inv_big[:, lo:hi], w_inv[:, lo:hi], SHIFT, None, ALU.mult).then_inc(w_scale_ready, 1)

            def gate_up_scales():
                for a in range(2):
                    if a == 1:
                        context_sums()
                    dve.wait_ge(wgu_in[a], 16 * FT)
                    last = v.tensor_reduce(w_max[:, a * FT:(a + 1) * FT], wgu_sb[:, a], AX.X, ALU.max,
                                           apply_absolute_value=True)
                step(last)
                weight_scales(0, 2 * FT)

            def down_weights():
                for t in range(KC):
                    dve.wait_ge(wd_in[t], 16)
                    last = v.tensor_reduce(w_max[:, 2 * FT + t:2 * FT + t + 1], wd_sb[:, t, :], AX.X, ALU.max,
                                           apply_absolute_value=True)
                step(last)
                weight_scales(2 * FT, 2 * FT + KC)
                statistics(0, 1)
                for t in range(KC):
                    i = 2 * FT + t
                    v.tensor_scalar(wd_val[:, t, :], wd_sb[:, t, :], w_inv[:, i:i + 1], 1.0, ALU.mult, ALU.mult
                                    ).then_inc(wd_over_scale, 1)
                dve.wait_ge(wd_scaled, KC)
                round_fp8(qwd[:, :, 0:FF], wd_val, wd_big, w_round, wd_over_scale, KC)

            def round_fp8(dst, val, big, ready, val_ready=None, count=0):
                step(v.tensor_scalar(big.bitcast(I32), big.bitcast(I32), EXP_BITS, HALF_BIT,
                                     ALU.bitwise_and, ALU.bitwise_or))
                if val_ready is not None:
                    dve.wait_ge(val_ready, count)
                step(v.scalar_tensor_tensor(val, big, M_LEAST, val, ALU.max, ALU.add))
                v.scalar_tensor_tensor(dst, big, M_LEAST, val, ALU.max, ALU.subtract).then_inc(ready, 1)

            def round_gate():
                dve.wait_ge(w_big_ready, FT)
                round_fp8(qgu[:, 0, :], wgu_sb[:, 0].rearrange("p t i -> p (t i)"), w_big[:, 0, :], w_round,
                          w_val_ready, FT)

            def up_magic():
                dve.wait_ge(w_big_ready, 2 * FT)
                big = w_big[:, 1, :].bitcast(I32)
                v.tensor_scalar(big, big, EXP_BITS, HALF_BIT, ALU.bitwise_and, ALU.bitwise_or).then_inc(up_step, 1)

            def up_sum(k):
                dve.wait_ge(w_val_ready, 2 * FT)
                dve.wait_ge(up_step, 1)
                cols = slice(k * FT // 2 * HID, (k + 1) * FT // 2 * HID)
                val = wgu_sb[:, 1].rearrange("p t i -> p (t i)")[:, cols]
                v.scalar_tensor_tensor(val, w_big[:, 1, cols], M_LEAST, val, ALU.max, ALU.add).then_inc(up_step, 1)

            def up_difference():
                dve.wait_ge(up_step, 3)
                v.scalar_tensor_tensor(qgu[:, 1, :], w_big[:, 1, :], M_LEAST,
                                       wgu_sb[:, 1].rearrange("p t i -> p (t i)"),
                                       ALU.max, ALU.subtract).then_inc(w_round, 1)

            def add_cross(h, u):
                dve.wait_ge(xm_ps, 2 * h + u + 1)
                n = h * SEQ + 2 * u
                dve.wait_ge(x1_out, 2 * h + u + 1)
                x1 = x1_sb[:, n:n + 2, :].rearrange("p n i -> p (n i)")
                v.tensor_tensor(x1, bank[XM_BANKS[h][u]][:, :], x1, ALU.add).then_inc(x2_ready, 1)

            def normalise_z2():
                dve.wait_ge(rstd_ready, 5)
                dve.wait_ge(x1_out, 2 * HALVES)
                for n in range(SEQ, SEQ + 3):
                    v.tensor_scalar(z2_sb[:, n, :], x1_sb[:, n, :], mv[:, 1, n, 0:1], rstd[:, 1, n:n + 1],
                                    ALU.subtract, ALU.mult).then_inc(z2_ready[0], 1)

            def z_scales(h):
                sl = slice(h * SEQ, (h + 1) * SEQ)
                dve.wait_ge(z3_ready[0], (h + 1) * 3)
                dve.wait_ge(z3_ready[1], h + 1)
                step(v.tensor_reduce(z_max[:, sl], z3_sb[:, sl, :], AX.X, ALU.max, apply_absolute_value=True))
                step(v.tensor_scalar(z_scale[:, sl], z_max[:, sl], 1.0 / FP8_MAX, None, ALU.mult))
                step(v.reciprocal(z_inv[:, sl], z_scale[:, sl]))
                v.tensor_scalar(z_inv_big[:, sl], z_inv[:, sl], SHIFT, None, ALU.mult).then_inc(z_inv_ready, 1)

            def round_z(h):
                sl = slice(h * SEQ, (h + 1) * SEQ)
                dve.wait_ge(z_big_ready, (h + 1) * SEQ)
                big = z_big[:, sl, :]
                step(v.tensor_scalar(big.bitcast(I32), big.bitcast(I32), EXP_BITS, HALF_BIT,
                                     ALU.bitwise_and, ALU.bitwise_or))
                dve.wait_ge(z_val_ready, (h + 1) * SEQ)
                step(v.scalar_tensor_tensor(z_val[:, sl, :], big, M_LEAST, z_val[:, sl, :], ALU.max, ALU.add))
                for lo, hi in ((h * SEQ, h * SEQ + 1), (h * SEQ + 1, (h + 1) * SEQ)):
                    v.scalar_tensor_tensor(qx[:, lo:hi, :], z_big[:, lo:hi, :], M_LEAST, z_val[:, lo:hi, :],
                                           ALU.max, ALU.subtract).then_inc(qx_ready, 1)

            def scale_gate(n):
                for k in range(2 if n < SHARED_FROM else 1):
                    i = 2 * n + k
                    cols = slice(k * FH, (k + 1) * FH)
                    dve.wait_ge(gate_ps, i + 1)
                    if n >= 2:
                        dve.wait_ge(silu_done, i - 3)
                    v.tensor_tensor(g1[:, n % 2, cols], bank[FFN_BANKS[k][0]][:, 0:FH],
                                    wsb_gu[:, 0, cols], ALU.mult).then_inc(g1_ready[k], 1)

            def activations(n):
                if n >= 2:
                    dve.wait_ge(qt_ready, n - 1)
                for k in range(2):
                    i = 2 * n + k
                    cols = slice(k * FH, (k + 1) * FH)
                    dve.wait_ge(up_ps, i + 1)
                    dve.wait_ge(sg_scaled, i + 1)
                    v.tensor_tensor(t_sb[:, n % 2, cols], bank[FFN_BANKS[k][1]][:, 0:FH], sg[:, n % 2, cols],
                                    ALU.mult).then_inc(t_ready, 1)

            def t_maximum(n):
                dve.wait_ge(t_ready, 2 * n + 2)
                v.tensor_reduce(t_max[:, n:n + 1], t_sb[:, n % 2, :], AX.X, ALU.max,
                                apply_absolute_value=True).then_inc(t_max_ready, 1)

            def t_scales(n):
                dve.wait_ge(t_max_ready, n + 1)
                v.tensor_scalar(t_scale[:, n, :], fp8_div[:, :], t_max[:, n:n + 1], None, ALU.mult
                                ).then_inc(t_scale_ready, 1)

            def t_inverse(n):
                dve.wait_ge(t_scale_ready, n + 1)
                v.reciprocal(t_inv[:, n, :], t_scale[:, n, :]).then_inc(t_inv_ready, 1)

            def magic_t(n):
                big = t_big[:, n % 2, :]
                dve.wait_ge(t_big_ready, n + 1)
                v.tensor_scalar(big.bitcast(I32), big.bitcast(I32), EXP_BITS, HALF_BIT,
                                ALU.bitwise_and, ALU.bitwise_or).then_inc(t_magic, 1)

            def sum_t(n, k):
                cols = slice(k * FH, (k + 1) * FH)
                dve.wait_ge(t_magic, n + 1)
                dve.wait_ge(t_val_ready, 2 * n + k + 1)
                v.scalar_tensor_tensor(t_val[:, n % 2, cols], t_big[:, n % 2, cols], M_LEAST,
                                       t_val[:, n % 2, cols], ALU.max, ALU.add).then_inc(t_sum, 1)

            def difference_t(n):
                b = n % 2
                dve.wait_ge(t_sum, 2 * n + 2)
                if n >= 2:
                    dve.wait_ge(qtT_ps, n - 1)
                for lo, hi in ((0, FF),) if n < NT - 1 else ((0, FPAD // 2), (FPAD // 2, FF)):
                    v.scalar_tensor_tensor(qt[:, b, lo:hi], t_big[:, b, lo:hi], M_LEAST, t_val[:, b, lo:hi],
                                           ALU.max, ALU.subtract).then_inc(qt_ready, 1)

            def last_output(n, down):
                dve.wait_ge(down_ps, n + 1)
                dve.wait_ge(o_scale_ready, n + 1)
                dve.wait_ge(y_ready, n - 1)
                step(v.scalar_tensor_tensor(o1[:, n % 2, :], down[:, 0:HID], o_scale[:, n:n + 1],
                                            wsb_d[:, :], ALU.mult, ALU.mult))
                v.tensor_tensor(y_sb[:, n, :], o1[:, n % 2, :], x2_sb[:, n, :], ALU.add).then_inc(y_last_ready, 1)

            statistics(0, 0)
            down_weights()
            query_key(0)
            probabilities(0)
            weighted_values(0, (1, 2))
            negate_maxima((0, 1))
            weighted_values(0, (3,))
            negate_maxima((2, 3))
            gate_up_scales()
            query_key(1)
            statistics(1, 0)
            probabilities(1)
            weighted_values(1, (1, 2, 3))
            round_gate()
            up_magic()
            add_cross(0, 0)
            up_sum(0)
            add_cross(0, 1)
            statistics(2, 0)
            up_sum(1)
            up_difference()
            z_scales(0)
            statistics(1, 1)
            round_z(0)
            normalise_z2()
            dve.wait_ge(tails_ready, 3)
            dve.wait_ge(wsb_out, 4)
            dve.wait_ge(consts_ready, 6)
            scale_gate(0)
            for n in range(NT):
                if n + 1 < NT:
                    scale_gate(n + 1)
                if n == 1:
                    add_cross(1, 0)
                    add_cross(1, 1)
                    statistics(2, 1)
                activations(n)
                if n == NT - 1:
                    t_maximum(n)
                    t_scales(n)
                    magic_t(n - 1)
                    t_inverse(n)
                    for k in range(2):
                        sum_t(n - 1, k)
                    difference_t(n - 1)
                    break
                if n >= 1:
                    magic_t(n - 1)
                t_maximum(n)
                if n == 2:
                    round_z(1)
                if n >= 1:
                    sum_t(n - 1, 0)
                t_scales(n)
                if n >= 1:
                    sum_t(n - 1, 1)
                t_inverse(n)
                if n >= 1:
                    difference_t(n - 1)
                if n == 1:
                    z_scales(1)
            magic_t(NT - 1)
            sum_t(NT - 1, 0)
            sum_t(NT - 1, 1)
            difference_t(NT - 1)
            last_output(NT - 2, bank[DOWN_BANK])
            last_output(NT - 1, bank[5])


_INS = ["x", "ctx_1024", "L0_attn_weight_qkv", "L0_attn_weight_proj", "L0_xattn_Wq", "L0_xattn_bq",
        "L0_xattn_Wk", "L0_xattn_bk", "L0_ffn_w_gate", "L0_ffn_w_up", "L0_ffn_w_down",
        "L0_ffn_down_reorder_index"]


def kernel(**inputs):
    import numpy as _np
    import concourse.bacc as _bacc
    from concourse import mybir as _mybir
    from concourse.bass_utils import run_bass_kernel_spmd as _run

    nc = _bacc.Bacc("TRN2", target_bir_lowering=False, num_devices=1)
    arrays, args = {}, []
    for name in _INS:
        a = _np.ascontiguousarray(inputs[name])
        arrays[f"in_{name}_dram"] = a
        args.append(nc.dram_tensor(f"in_{name}_dram", a.shape, _mybir.dt.from_np(a.dtype), kind="ExternalInput").ap())
    args.append(nc.dram_tensor("out_0_dram", inputs["x"].shape, _mybir.dt.float32, kind="ExternalOutput").ap())
    decoder_layer_kernel(nc, *args)
    r = _run(nc, [arrays], core_ids=[0])
    return r.results[0]["out_0_dram"]
```
